# Optimizing a Trainium2 kernel written in Bass

```python
import numpy as np
import jax
import jax.numpy as jnp

def _softmax(x, axis=-1):
    return jax.nn.softmax(x, axis=axis)

def _gelu(x):
    return jax.nn.gelu(x, approximate=True)

def _silu(x):
    return jax.nn.silu(x)

def _sigmoid(x):
    return jax.nn.sigmoid(x)

def _layernorm(x, axis=-1, eps=1e-05):
    m = jnp.mean(x, axis=axis, keepdims=True)
    v = jnp.var(x, axis=axis, keepdims=True)
    return (x - m) / jnp.sqrt(v + eps)

def _scatter_add(tgt, idx, src, axis=0):
    return tgt.at[idx].add(src)

def _segment_sum(src, seg, n):
    return jax.ops.segment_sum(src, seg, n)
kernel_name = 'mk_adaln_d1_jaxref_r4_60af2d'

def setup_inputs(seed: int=0):
    np.random.seed(seed)
    _w = jnp.asarray

    def _L0_attn_setup():
        import jax, jax.numpy as jnp
        import numpy as np
        import math
        EPS = 1e-06

        def favorplus_features(x, proj):
            xw = jnp.einsum('bhtd,hmd->bhtm', x, proj)
            xw = xw - jnp.max(xw, axis=-1, keepdims=True)
            x_norm_sq = jnp.sum(x * x, axis=-1, keepdims=True)
            return jnp.exp(xw) * jnp.exp(-0.5 * x_norm_sq) + EPS
        key = jax.random.key(seed)
        ks = jax.random.split(key, 6)
        B, T, d = (2, 1024, 256)
        h, m = (16, 64)
        dk = d // h
        s = 1.0 / math.sqrt(d)
        return {'x': jax.random.normal(ks[0], (B, T, d), dtype=jnp.float32), 'Wq': jax.random.normal(ks[1], (d, d), dtype=jnp.float32) * s, 'Wk': jax.random.normal(ks[2], (d, d), dtype=jnp.float32) * s, 'Wv': jax.random.normal(ks[3], (d, d), dtype=jnp.float32) * s, 'Wo': jax.random.normal(ks[4], (d, d), dtype=jnp.float32) * s, 'bo': jnp.zeros((d,), dtype=jnp.float32), 'proj': jax.random.normal(ks[5], (h, m, dk), dtype=jnp.float32)}
    _L0_attn_in = _L0_attn_setup()

    def _L0_ffn_setup():
        import jax, jax.numpy as jnp
        import numpy as np
        B, T, D, E, H = (4, 512, 256, 4, 8)
        EPS = 1e-05

        def _uniform(k, shape, bound):
            return jax.random.uniform(k, shape, jnp.float32, -bound, bound)

        def _layernorm(x, w, b):
            mu = jnp.mean(x, axis=-1, keepdims=True)
            var = jnp.mean(jnp.square(x - mu), axis=-1, keepdims=True)
            return (x - mu) * jax.lax.rsqrt(var + EPS) * w + b
        key = jax.random.key(seed)
        ks = jax.random.split(key, 12)
        wb = np.sqrt(6.0 / D) / np.sqrt(6.0)
        wb = 1.0 / np.sqrt(D)
        return {'x': jax.random.normal(ks[0], (B, T, D), jnp.float32), 'router_prob': jax.random.uniform(ks[1], (B, T, E), jnp.float32), 'norm_w': jnp.ones((D,), jnp.float32), 'norm_b': jnp.zeros((D,), jnp.float32), 'q_w': _uniform(ks[2], (D, D), wb), 'q_b': _uniform(ks[3], (D,), wb), 'k_w': _uniform(ks[4], (D, D), wb), 'k_b': _uniform(ks[5], (D,), wb), 'v_w': _uniform(ks[6], (D, D), wb), 'v_b': _uniform(ks[7], (D,), wb), 'o_w': _uniform(ks[8], (D, D), wb), 'o_b': _uniform(ks[9], (D,), wb)}
    _L0_ffn_in = _L0_ffn_setup()
    _L0_c = _w((lambda *s: np.random.randn(*s).astype(np.float32) * 0.05)(4, 256))
    _L0_wmod = _w((lambda *s: np.random.randn(*s).astype(np.float32) * 0.05)(256, 6 * 256) * 256 ** (-0.5))
    _d = {'L0_attn_x': _L0_attn_in['x'], 'L0_attn_Wq': _L0_attn_in['Wq'], 'L0_attn_Wk': _L0_attn_in['Wk'], 'L0_attn_Wv': _L0_attn_in['Wv'], 'L0_attn_Wo': _L0_attn_in['Wo'], 'L0_attn_bo': _L0_attn_in['bo'], 'L0_attn_proj': _L0_attn_in['proj'], 'L0_ffn_router_prob': _L0_ffn_in['router_prob'], 'L0_ffn_norm_w': _L0_ffn_in['norm_w'], 'L0_ffn_norm_b': _L0_ffn_in['norm_b'], 'L0_ffn_q_w': _L0_ffn_in['q_w'], 'L0_ffn_q_b': _L0_ffn_in['q_b'], 'L0_ffn_k_w': _L0_ffn_in['k_w'], 'L0_ffn_k_b': _L0_ffn_in['k_b'], 'L0_ffn_v_w': _L0_ffn_in['v_w'], 'L0_ffn_v_b': _L0_ffn_in['v_b'], 'L0_ffn_o_w': _L0_ffn_in['o_w'], 'L0_ffn_o_b': _L0_ffn_in['o_b'], 'L0_c': _L0_c, 'L0_wmod': _L0_wmod}
    _x0 = _d['L0_attn_x']
    _d['L0_attn_x'] = jax.random.normal(jax.random.fold_in(jax.random.key(seed), 1), (4, 2048, 256), dtype=_x0.dtype)
    del _x0
    return _d

def reference(L0_attn_x, L0_attn_Wq, L0_attn_Wk, L0_attn_Wv, L0_attn_Wo, L0_attn_bo, L0_attn_proj, L0_ffn_router_prob, L0_ffn_norm_w, L0_ffn_norm_b, L0_ffn_q_w, L0_ffn_q_b, L0_ffn_k_w, L0_ffn_k_b, L0_ffn_v_w, L0_ffn_v_b, L0_ffn_o_w, L0_ffn_o_b, L0_c, L0_wmod):

    def _L0_attn_ref(x, Wq, Wk, Wv, Wo, bo, proj):
        import jax, jax.numpy as jnp
        import numpy as np
        import math
        EPS = 1e-06

        def favorplus_features(x, proj):
            xw = jnp.einsum('bhtd,hmd->bhtm', x, proj)
            xw = xw - jnp.max(xw, axis=-1, keepdims=True)
            x_norm_sq = jnp.sum(x * x, axis=-1, keepdims=True)
            return jnp.exp(xw) * jnp.exp(-0.5 * x_norm_sq) + EPS
        B, T, d = x.shape
        h, m, dk = proj.shape

        def heads(W):
            y = jnp.einsum('btd,ed->bte', x, W)
            return y.reshape(B, T, h, dk).transpose(0, 2, 1, 3)
        Q = heads(Wq) / math.sqrt(dk)
        K = heads(Wk) / math.sqrt(dk)
        V = heads(Wv)
        inv_sqrt_m = 1.0 / math.sqrt(m)
        phiQ = favorplus_features(Q, proj) * inv_sqrt_m
        phiK = favorplus_features(K, proj) * inv_sqrt_m
        KV = jnp.einsum('bhtm,bhtd->bhmd', phiK, V)
        Ksum = jnp.sum(phiK, axis=2)
        num = jnp.einsum('bhtm,bhmd->bhtd', phiQ, KV)
        den = jnp.einsum('bhtm,bhm->bht', phiQ, Ksum)[..., None] + EPS
        out_heads = num / den
        merged = out_heads.transpose(0, 2, 1, 3).reshape(B, T, d)
        return jnp.einsum('btd,ed->bte', merged, Wo) + bo

    def _L0_ffn_ref(x, router_prob, norm_w, norm_b, q_w, q_b, k_w, k_b, v_w, v_b, o_w, o_b):
        import jax, jax.numpy as jnp
        import numpy as np
        B, T, D, E, H = (4, 512, 256, 4, 8)
        EPS = 1e-05

        def _uniform(k, shape, bound):
            return jax.random.uniform(k, shape, jnp.float32, -bound, bound)

        def _layernorm(x, w, b):
            mu = jnp.mean(x, axis=-1, keepdims=True)
            var = jnp.mean(jnp.square(x - mu), axis=-1, keepdims=True)
            return (x - mu) * jax.lax.rsqrt(var + EPS) * w + b
        e_cnt = router_prob.shape[2]
        b, t, d = x.shape
        n = t // e_cnt
        h = H
        scale = d ** (-0.5)
        qs, ks_, vs = ([], [], [])
        for e in range(e_cnt):
            xe = x[:, e * n:(e + 1) * n, :]
            xn = _layernorm(xe, norm_w, norm_b)
            m = d // 2 ** e
            xm = xn[..., :m]
            qs.append(jnp.einsum('bnm,dm->bnd', xm, q_w[:, :m]) + q_b)
            ks_.append(jnp.einsum('bnm,dm->bnd', xm, k_w[:, :m]) + k_b)
            vs.append(jnp.einsum('bnm,dm->bnd', xm, v_w[:, :m]) + v_b)
        q = jnp.concatenate(qs, axis=1)
        k = jnp.concatenate(ks_, axis=1)
        v = jnp.concatenate(vs, axis=1)
        dh = d // h
        q = q.reshape(b, t, h, dh).transpose(0, 2, 1, 3)
        k = k.reshape(b, t, h, dh).transpose(0, 2, 1, 3)
        v = v.reshape(b, t, h, dh).transpose(0, 2, 1, 3)
        attn = jnp.einsum('bhqd,bhkd->bhqk', q, k) * scale
        attn = jax.nn.softmax(attn, axis=-1)
        attn_out = jnp.einsum('bhqk,bhkd->bhqd', attn, v)
        attn_out = attn_out.transpose(0, 2, 1, 3).reshape(b, t, d)
        outs = []
        for e in range(e_cnt):
            sl = slice(e * n, (e + 1) * n)
            m = d // 2 ** e
            xm = attn_out[:, sl, :m]
            out = jnp.einsum('bnm,om->bno', xm, o_w[:m, :m]) + o_b[:m]
            pad = d - m
            if pad:
                out = jnp.pad(out, ((0, 0), (0, 0), (0, pad)))
            outs.append(out + x[:, sl, :])
        return jnp.concatenate(outs, axis=1)
    x = L0_attn_x
    mod = (_silu(L0_c) @ L0_wmod).reshape(L0_c.shape[0], 6, 1, -1)
    sa, ca, ga, sb, cb, gb = (mod[:, 0], mod[:, 1], mod[:, 2], mod[:, 3], mod[:, 4], mod[:, 5])
    ga = (2 * (ga >= 0) - 1) * jnp.maximum(jnp.abs(ga), 0.25)
    gb = (2 * (gb >= 0) - 1) * jnp.maximum(jnp.abs(gb), 0.25)
    h = _layernorm(x, axis=-1) * (1 + ca) + sa
    x = x + ga * _L0_attn_ref(h, L0_attn_Wq, L0_attn_Wk, L0_attn_Wv, L0_attn_Wo, L0_attn_bo, L0_attn_proj)
    h = _layernorm(x, axis=-1) * (1 + cb) + sb
    x = x + gb * _L0_ffn_ref(h, L0_ffn_router_prob, L0_ffn_norm_w, L0_ffn_norm_b, L0_ffn_q_w, L0_ffn_q_b, L0_ffn_k_w, L0_ffn_k_b, L0_ffn_v_w, L0_ffn_v_b, L0_ffn_o_w, L0_ffn_o_b)
    return x

_drawn_inputs = setup_inputs


def setup_inputs(seed=0):
    import zlib

    import numpy as np

    out = dict(_drawn_inputs(seed))
    spreads = {'L0_attn_bo': (0.0, 0.332), 'L0_ffn_norm_w': (1.0, 0.6), 'L0_ffn_norm_b': (0.0, 0.8)}
    factors = {'L0_attn_Wq': 38.233,
     'L0_attn_Wk': 33.571,
     'L0_attn_Wv': 33.654,
     'L0_attn_Wo': 35.13,
     'L0_attn_proj': 38.884,
     'L0_ffn_q_w': 8.0,
     'L0_ffn_q_b': 8.0,
     'L0_ffn_k_w': 8.0,
     'L0_ffn_k_b': 64.0,
     'L0_ffn_v_w': 8.0,
     'L0_ffn_v_b': 8.0,
     'L0_ffn_o_w': 8.0,
     'L0_ffn_o_b': 44.706}
    for name, (base, spread) in spreads.items():
        noise = np.random.default_rng([zlib.crc32(name.encode()), seed]).standard_normal(out[name].shape)
        drawn = base * np.exp(spread * noise) if base else spread * noise
        out[name] = jnp.asarray(drawn.astype(out[name].dtype))
    for name, factor in factors.items():
        out[name] = (out[name] * factor).astype(out[name].dtype)
    return out
```

```python
from contextlib import ExitStack

import concourse.bass as bass
from concourse import mybir

F32 = mybir.dt.float32
F32R = mybir.dt.float32r
ALU = mybir.AluOpType
ACT = mybir.ActivationFunctionType
AX = mybir.AxisListType

P = 128
CH = 512
TPC = CH // P

FAVOR_EPS = 1e-6
NORM_EPS = 1e-5
FLOOR = 0.25


class Chain:

    def __init__(self, eng, sem, passed=None):
        self.passed = passed
        self.eng, self.sem, self.base, self.n, self.outer = eng, sem, 0, 0, []

    def __call__(self, ins):
        ins.then_inc(self.sem, 1)
        self.n += 1
        self.eng.wait_ge(self.sem, self.base + self.n)
        if self.passed is not None:
            self.eng.sem_inc(self.passed, 1)

    def enter(self, i, per):
        self.outer.append((self.base, self.n, per))
        self.base, self.n = self.base + self.n + i * per, 0

    def leave(self, trips):
        assert self.n == self.outer[-1][2], self.n
        self.base, n, per = self.outer.pop()
        self.n = n + per * trips


def adaln_block(nc, x, Wq, Wk, Wv, Wo, bo, proj, norm_w, norm_b, q_w, q_b, k_w, k_b, v_w, v_b, o_w, o_b,
                cond, wmod, out):
    B, T, D = x.shape
    NH, NM, DK = proj.shape
    H2N, EXPERTS = 8, 4
    DH = D // H2N
    KD = D // P
    NT, NC = T // P, T // CH
    GR = NH * NM // P
    EV = DK + 1
    assert NC == EXPERTS and NT == NC * TPC and KD == 2 and GR == 8
    PHI = 1.0 / NM ** 0.5
    QS = 1.0 / DK ** 0.5
    SCALE = float(D) ** -0.5
    width = [D >> e for e in range(EXPERTS)]

    units = [(h, c) for h in range(H2N) for c in range(NC) if h * DH < width[c]]
    NU = len(units)
    KT = T // P
    STEPS = KT // 2
    MAXU = TPC * NC
    loads_of = {}
    for u, (h, c) in enumerate(units):
        loads_of.setdefault(h, u)

    NQ = 3 * NC + 1
    QSN = [len(range(i, NQ, 3)) for i in range(3)]
    SHN = [len(range(i, NU, 4)) for i in range(4)]
    LOOK = MAXU * 3 // 2
    expert = [(s + 1) % NC for s in range(NC)]
    slot_of = {e: s for s, e in enumerate(expert)}
    RECIPROCALS = ((3, 5), (2, 8), (0, 11), (1, 12))
    OUT_STEPS = (2, 4, 6)
    PER_B, PER_C, PER_P = 207, 24, 10


    k_scr = nc.dram_tensor("k_scr", (2, D, T), F32, kind="Internal").ap()
    q_scr = nc.dram_tensor("q_scr", (2, D, T), F32, kind="Internal").ap()

    with ExitStack() as ctx:
        def sb(name, shape, dt=F32, stack=ctx):
            return stack.enter_context(nc.sbuf_tensor(name, shape, dt))

        def sem(name):
            return ctx.enter_context(nc.semaphore(name))

        X = sb("X", [P, NT, D])
        W1T = sb("W1T", [P, KD, 3 * D])
        WoT = sb("WoT", [P, KD, D])
        WoG, BOG = sb("WoG", [P, KD, D]), sb("BOG", [P, D])
        W2T = sb("W2T", [P, KD, 3 * D])
        W2M = sb("W2M", [P, 2, 3 * D])
        OWT = sb("OWT", [P, KD, D])
        OWM = sb("OWM", [P, 2, 64])
        OWG, OWMG = sb("OWG", [P, KD, D]), sb("OWMG", [P, 2, 64])
        PB = sb("PB", [P, 2, CH])
        MODB = sb("MODB", [P, B, 4, D])
        MODC = sb("MODC", [P, 2, KD, B])
        BO, VB, OB = sb("BO", [P, D]), sb("VB", [P, D]), sb("OB", [P, D])
        COLS = sb("COLS", [P, 4, KD])
        QBS = sb("QBS", [P, KD])
        ident = sb("ident", [P, P])
        ones = sb("ones", [P, DH])
        minus_half = sb("minus_half", [P, NT])
        STAT = sb("STAT", [P, NT, 6])
        MV = sb("MV", [P, NT, 2])
        VE = sb("VE", [P, NT])
        RSTD = sb("RSTD", [P, NT])
        KVS = sb("KVS", [P, GR, 2 * EV])
        NW, DW = sb("NW", [P, GR, 32]), sb("DW", [P, GR, 32])

        s0 = ExitStack()
        WN = sb("WN", [P, 8, KD, D], stack=s0)
        PN = sb("PN", [P, GR, P], stack=s0)
        WM = sb("WM", [P, KD, 6 * D], stack=s0)
        CT = sb("CT", [P, KD, B], stack=s0)
        CE = sb("CE", [P, KD, B], stack=s0)
        SC = sb("SC", [P, KD, B], stack=s0)
        SCB = sb("SCB", [P, KD, B, P], stack=s0)
        GS = sb("GS", [P, B, 2, D], stack=s0)
        s0.close()

        s1 = ExitStack()
        QOP = sb("QOP", [97, 4, CH], F32R, stack=s1)
        KOP = sb("KOP", [97, 4, T], F32R, stack=s1)
        PR = sb("PR", [P, 2, 2, CH], stack=s1)
        CS = sb("CS", [2 * DH, 2, CH], stack=s1)
        SUM = sb("SUM", [P, NC + 1, CH], stack=s1)
        s1.close()
        PHIQ = sb("PHIQ", [P, GR, T])

        s2 = ExitStack()
        XH = sb("XH", [P, TPC, D], stack=s2)
        HT = sb("HT", [P, KD, CH], stack=s2)
        QK = sb("QK", [P, 2, 2 * D], stack=s2)
        SQ = sb("SQ", [P, 2, 2 * D], stack=s2)
        N2 = sb("N2", [P, TPC, 2 * NH], stack=s2)
        QKT = sb("QKT", [P, TPC, 4, P], stack=s2)
        MXK, MXQ = sb("MXK", [P, NH], stack=s2), sb("MXQ", [P, NH], stack=s2)
        XSK = sb("XSK", [P, NH * NM], stack=s2)
        XSQ = sb("XSQ", [P, NH * NM], stack=s2)
        PK = sb("PK", [P, 2, NH * NM], stack=s2)
        V1 = sb("V1", [P, TPC, NH, EV], stack=s2)
        s2.close()

        V2 = sb("V2", [P, KT, D])
        Hh = sb("Hh", [P, NT, D])
        X2 = sb("X2", [P, TPC, D])
        XNT = sb("XNT", [P, KD, CH])
        TMP = sb("TMP", [P, 2, CH])
        QKS = sb("QKS", [P, 3, 2, CH], F32R)
        MXP = sb("MXP", [P, 2, TPC, NC])
        MXN = sb("MXN", [P, 2, 32])
        MXT = sb("MXT", [P, 2, 32])
        s3 = ExitStack()
        NUM = sb("NUM", [P, NC + 1, CH], stack=s3)
        s3.close()
        DENS = sb("DENS", [P, CH])
        NUMS = sb("NUMS", [P, 2, CH])
        R = sb("R", [P, TPC, 4, 4])
        RB = sb("RB", [P, 2, TPC, P])
        MT = sb("MT", [P, 2, CH])

        PS = ctx.enter_context(nc.psum_tensor("PS", [P, 8, CH], F32))

        def bank(i, n=1):
            return PS[:, i:i + n, :].rearrange("p b n -> p (b n)")

        def out_ps(e):
            if e == 0:
                return bank(4, 2)
            return bank(0) if e == 1 else bank(1)[:, (0 if e == 2 else 4 * width[2]):][:, 0:TPC * width[e]]

        names = """w_in c_in vec_in pj_in id0 id_ok nb0 mh_ok mk0
                   wT wT_sb pT pT_sb sig sc_ok mod mod_sb setup_ok
                   x_first x_rest ve1 rstd1 xh xT hT qkv qk_sb sq v_sb n2 qkT qkT_sb xwk xwq xk_sb xq_sb expk expq
                   phik kv kv_sb eqt phiq v1_ones gated xb kw_ok
                   den den_sb num num_sb denT rb rT mt yps x1
                   ve2 rstd2 ve3 rstd3 h2a h2m h2 x2 x2T xn_sb qp q_tmp q_hi q_lo scr0 scr1 scr2 vp v2_sb init_ok
                   q_in0 q_in1 q_in2 q_in3 k_in0 k_in1 k_in2 k_in3 am am_rd mxt shift0 shift1 shift2 shift3
                   sc_b ex cps cs_up c_out pool_own rcp at at_last base ops fin st0 st1 st2 st3 fin_n dve_own passed""".split()
        S = {n: sem(n) for n in names}
        from_one = "xT xk_sb xq_sb phiq kv kv_sb n2 qkT_sb phik eqt".split()
        q_in = [S[f"q_in{i}"] for i in range(4)]
        k_in = [S[f"k_in{i}"] for i in range(4)]
        shift = [S[f"shift{i}"] for i in range(4)]

        block = ctx.enter_context(nc.Block())
        xv = x.rearrange("b (c t p) d -> p (b c) t d", p=P, t=TPC)
        ov = out.rearrange("b (c t p) d -> p (b c) t d", p=P, t=TPC)
        heads = sorted(loads_of)
        last_unit = {h: max(u for u, (hh, _) in enumerate(units) if hh == h) for h in heads}
        scr = [S[f"scr{i}"] for i in range(3)]
        st = [S[f"st{i}"] for i in range(NC)]

        def slot(s):
            return slice(s * TPC, (s + 1) * TPC)

        def blocks(s):
            return [(3 * s + t, t) for t in ((0, 1, 2, 3) if expert[s] == 0 else (0, 1, 2))]

        def stored(b, n):
            return scr[n % 3], 32 * (QSN[n % 3] * b + n // 3 + 1)

        def wait_apart(eng, *waits):
            for s_, value in waits:
                eng.wait_ge(s_, value)
                eng.sem_inc(S["passed"], 1)

        @block.sync
        def _(sp):
            for w, src in enumerate((Wq, Wk, Wv, Wo, q_w, k_w, v_w, o_w)):
                sp.dma_start(WN[:, w], src.rearrange("(e p) d -> p e d", p=P)).then_inc(S["w_in"], 16)
            sp.dma_start(WM[:], wmod.rearrange("(k p) n -> p k n", p=P)).then_inc(S["c_in"], 16)
            for k in range(KD):
                sp.dma_start(CT[:, k], cond[:, k * P:(k + 1) * P].rearrange("b p -> p b"),
                             allow_slow_non_contiguous=True).then_inc(S["c_in"], 16)
            for dst, src in ((BO, bo), (VB, v_b), (OB, o_b)):
                sp.dma_start(dst[:], src.rearrange("(a n) -> a n", a=1).broadcast_to([P, D])).then_inc(S["vec_in"], 16)
            for n, src in enumerate((norm_w, norm_b, q_b, k_b)):
                sp.dma_start(COLS[:, n], src.rearrange("(k p) -> p k", p=P),
                             allow_slow_non_contiguous=True).then_inc(S["vec_in"], 16)
            sp.wait_ge(S["nb0"], 1)
            for h in range(NH):
                r, c = h % 2 * NM, h % 8 * DK
                sp.dma_start(PN[r:r + NM, h // 2, c:c + DK], proj[h]).then_inc(S["pj_in"], 16)

            def load_x(b, s):
                sp.dma_start(X[:, slot(s)], xv[:, bass.ds(b * NC + expert[s], 1)].rearrange("p o t d -> p (o t) d")
                             ).then_inc(S["x_first" if s == 0 else "x_rest"], 16)

            for s in range(NC):
                load_x(0, s)

            def batch(b, last):
                for s in range(NC):
                    e = expert[s]
                    for n, t in blocks(s):
                        dst, j = (k_scr, t) if t < 2 else (q_scr, t - 2)
                        sp.wait_ge(S["q_lo"], NQ * b + n + 1)
                        for half in range(2):
                            sp.dma_start(dst[half, j * P:(j + 1) * P, e * CH:(e + 1) * CH],
                                         QKS[:, n % 3, half].bitcast(F32)).then_inc(scr[n % 3], 16)

                def load_k(h):
                    s = heads.index(h) % 4
                    for r, half in ((0, 0), (32, 0), (64, 1)):
                        sp.dma_start(KOP[r:r + DH, s].bitcast(F32),
                                     k_scr[half, h * DH:(h + 1) * DH, :]).then_inc(k_in[s], 16)

                def load_q(u):
                    h, c = units[u]
                    for r, half in ((0, 0), (32, 1), (64, 0)):
                        sp.dma_start(QOP[r:r + DH, u % 4].bitcast(F32),
                                     q_scr[half, h * DH:(h + 1) * DH, c * CH:(c + 1) * CH]).then_inc(q_in[u % 4], 16)

                def load_shift(u):
                    sp.wait_ge(S["mxt"], NU * b + u + 1)
                    for g in range(4):
                        dst = QOP[96:97, u % 4, :].bitcast(F32).rearrange("o (t g n) -> o t g n", t=TPC, g=4)[:, :, g]
                        sp.dma_start(dst, MXT[32 * g:32 * g + TPC, u % 2, :]).then_inc(shift[u % 4], 16)

                wait_apart(sp, *[stored(b, n) for n in range(NQ - 3, NQ)], (S["init_ok"], b + 1))
                loaded_k = set()
                for u in range(4):
                    h = units[u][0]
                    if h not in loaded_k:
                        load_k(h)
                        loaded_k.add(h)
                    load_q(u)
                for h in heads[1:4]:
                    if h not in loaded_k:
                        load_k(h)
                        loaded_k.add(h)
                load_shift(0)
                for u in range(NU):
                    if u + 1 < NU:
                        load_shift(u + 1)
                    if u < NU - 1:
                        wait_apart(sp, (S["sc_b"], STEPS * (NU * b + u + 1)))
                    if u + 4 < NU:
                        load_q(u + 4)
                    for h in heads[4:]:
                        if h not in loaded_k and last_unit[heads[heads.index(h) - 4]] <= u:
                            load_k(h)
                            loaded_k.add(h)
                for s in range(NC):
                    sp.wait_ge(S["fin"], NC * b + s + 1)
                    sp.dma_start(ov[:, bass.ds(b * NC + expert[s], 1)].rearrange("p o t d -> p (o t) d"),
                                 X[:, slot(s)]).then_inc(st[s], 16)
                    if s > 0 and not last:
                        wait_apart(sp, (st[s - 1], 16 * (b + 1)))
                        load_x(b + 1, s - 1)
                if not last:
                    wait_apart(sp, (st[NC - 1], 16 * (b + 1)))
                    load_x(b + 1, NC - 1)

            with sp.Fori(0, B - 1) as b:
                batch(b, False)
            batch(B - 1, True)
            for s in range(NC):
                sp.wait_ge(st[s], 16 * B)

        @block.gpsimd
        def _(pool):
            g = nc.gpsimd
            for n in from_one:
                pool.sem_inc(S[n], 1)
            g.memset(PN[:], 0.0).then_inc(S["nb0"], 1)
            g.memset(ident[:], 0.0).then_inc(S["id0"], 1)
            pool.wait_ge(S["id0"], 1)
            g.affine_select(out=ident[:], in_=ident[:], compare_op=ALU.not_equal, fill=1.0, base=0,
                            pattern=[[-1, P]], channel_multiplier=1).then_inc(S["id_ok"], 1)
            g.memset(minus_half[:], -0.5).then_inc(S["mh_ok"], 1)
            g.memset(ones[:], 1.0).then_inc(S["mh_ok"], 1)
            g.memset(W2M[:], 0.0).then_inc(S["mk0"], 1)
            g.memset(OWM[:], 0.0).then_inc(S["mk0"], 1)
            pool.wait_ge(S["mh_ok"], 2)
            pool.wait_ge(S["setup_ok"], 1)
            with pool.Fori(0, B) as b:
                def rsqrt(cols, ready, signal, n):
                    wait_apart(pool, (S[ready], n))
                    g.tensor_tensor(RSTD[:, cols], VE[:, cols], minus_half[:, cols], ALU.pow).then_inc(S[signal], 1)

                g.memset(V1[:, :, :, DK:EV], 1.0).then_inc(S["v1_ones"], 1)
                rsqrt(slot(0), "ve1", "rstd1", NC * b + 1)
                gate = MODB[:, bass.ds(b, 1), 0, :]
                g.tensor_tensor(WoG[:], WoT[:], gate.broadcast_to([P, KD, D]), ALU.mult).then_inc(S["gated"], 1)
                g.tensor_tensor(BOG[:], BO[:], gate.rearrange("p o d -> p (o d)"), ALU.mult).then_inc(S["gated"], 1)

                def chunk(s, last):
                    t0 = (b * NC + s) * TPC
                    for i in range(TPC):
                        if i == 2 and not last:
                            rsqrt(slot(0), "ve1", "rstd1", b * NC + s + 2)
                        wait_apart(pool, (S["expk"], t0 + i + 1), (S["kv"], 1 + (t0 if i < 2 else t0 + i - 1)))
                        g.tensor_scalar(PK[:, i % 2], XSK[:], FAVOR_EPS, PHI, ALU.add, ALU.mult).then_inc(S["phik"], 1)
                    wait_apart(pool, (S["xh"], t0 + TPC), (S["gated"], 2 * (b + 1)))
                    sl = bass.ds(s * TPC, TPC)
                    g.tensor_tensor(X[:, sl], X[:, sl], BOG[:].rearrange("p (o d) -> p o d", o=1)
                                    .broadcast_to([P, TPC, D]), ALU.add).then_inc(S["xb"], 1)

                with pool.Fori(0, NC - 1) as s:
                    chunk(s, False)
                chunk(NC - 1, True)
                for s in range(NC + 1):
                    if s < NC:
                        rsqrt(slot(s), "ve2", "rstd2", NC * b + s + 1)
                    if s >= 1:
                        rsqrt(slot(s - 1), "ve3", "rstd3", NC * b + s)
                    if s < NC:
                        for op, m, ready, signal in ((ALU.mult, 2, "h2a", "h2m"), (ALU.add, 1, "h2m", "h2")):
                            wait_apart(pool, (S[ready], NC * b + s + 1))
                            g.tensor_tensor(Hh[:, slot(s)], Hh[:, slot(s)],
                                            MODB[:, bass.ds(b, 1), m, :].broadcast_to([P, TPC, D]), op
                                            ).then_inc(S[signal], 1)
                wait_apart(pool, (S["num"], NC * (b + 1)), (S["rstd3"], NC * (b + 1)))
                g.memset(KOP[96:97].bitcast(F32), 1.0).then_inc(S["init_ok"], 1)

                wait_apart(pool, (S["x2"], NT * (b + 1)), (S["init_ok"], b + 1))
                own_g = Chain(pool, S["pool_own"], S["passed"])
                own_g.enter(b, PER_P)
                gate = MODB[:, bass.ds(b, 1), 3, :]
                own_g(g.tensor_tensor(OWG[:], OWT[:], gate.broadcast_to([P, KD, D]), ALU.mult))
                own_g(g.tensor_tensor(OWMG[:], OWM[:], gate[:, :, 0:64].broadcast_to([P, 2, 64]), ALU.mult))
                for s in range(NC):
                    m = width[expert[s]]
                    own_g(g.tensor_tensor(Hh[:, slot(s), 0:m], Hh[:, slot(s), 0:m], OB[:, 0:m]
                                          .rearrange("p (o d) -> p o d", o=1).broadcast_to([P, TPC, m]), ALU.add))
                    own_g(g.tensor_tensor(Hh[:, slot(s)], Hh[:, slot(s)], gate.broadcast_to([P, TPC, D]), ALU.mult))
                    g.tensor_tensor(X[:, slot(s)], X[:, slot(s)], Hh[:, slot(s)], ALU.add).then_inc(S["base"], 1)
                own_g.leave(B)
                for k, (z, _) in enumerate(RECIPROCALS):
                    wait_apart(pool, (S["rcp"], TPC * (len(RECIPROCALS) * b + k + 1)))
                    g.tensor_tensor(NUM[:, z], NUM[:, z], SUM[:, z], ALU.mult).then_inc(S["at"], 1)
                wait_apart(pool, (S["fin"], NC * (b + 1)))

        @block.scalar
        def _(act):
            a = nc.scalar
            act.wait_ge(S["c_in"], 16 * (1 + KD))
            a.activation(CE[:], CT[:], ACT.Exp, scale=-1.0).then_inc(S["sig"], 1)
            act.wait_ge(S["setup_ok"], 1)
            with act.Fori(0, B) as b:
                def modulated(g):
                    wait_apart(act, (S["xT"], 1 + g + 1))
                    for k in range(KD):
                        a.activation(HT[:, k], bank(k), ACT.Identity, bias=MODC[:, 0, k, bass.ds(b, 1)],
                                     scale=MODC[:, 1, k, bass.ds(b, 1)]).then_inc(S["hT"], 1)

                def chunk(s, last):
                    g = b * NC + s
                    t0 = g * TPC

                    def qkt(i):
                        act.wait_ge(S["qkT"], t0 + i + 1)
                        a.activation(QKT[:, i].rearrange("p a n -> p (a n)"), bank(6), ACT.Copy).then_inc(S["qkT_sb"], 1)

                    for i in range(TPC):
                        act.wait_ge(S["qkv"], t0 + i + 1)
                        src = bank(2 + i % 2 * 2)
                        a.activation(QK[:, i % 2], src, ACT.Copy).then_inc(S["qk_sb"], 1)
                        act.wait_ge(S["n2"], 1 + (t0 if i < 2 else t0 + i - 1))
                        a.activation(SQ[:, i % 2], src, ACT.Square).then_inc(S["sq"], 1)
                        if i >= 1:
                            qkt(i - 1)
                    qkt(TPC - 1)

                    def phiq(i):
                        act.wait_ge(S["eqt"], 1 + t0 + i + 1)
                        a.activation(PHIQ[:, :, bass.ds(s * CH + i * P, P)], bank(4, 2).rearrange("p (g n) -> p g n", g=GR),
                                     ACT.Copy, bias=FAVOR_EPS * PHI, scale=PHI).then_inc(S["phiq"], 1)

                    for i in range(TPC):
                        act.wait_ge(S["xk_sb"], 1 + t0 + i + 1)
                        a.activation(XSK[:], XSK[:], ACT.Exp).then_inc(S["expk"], 1)
                        act.wait_ge(S["xq_sb"], 1 + t0 + i + 1)
                        a.activation(XSQ[:], XSQ[:], ACT.Exp).then_inc(S["expq"], 1)
                        if i >= 1:
                            phiq(i - 1)
                    if not last:
                        modulated(g + 1)
                    phiq(TPC - 1)

                modulated(b * NC)
                with act.Fori(0, NC - 1) as s:
                    chunk(s, False)
                chunk(NC - 1, True)

                for it in range(NC + 2):
                    if it < NC:
                        g = b * NC + it
                        act.wait_ge(S["den"], g + 1)
                        if it > 0:
                            act.wait_ge(S["denT"], g)
                        a.activation(DENS[:], bank(6), ACT.Copy).then_inc(S["den_sb"], 1)
                        act.wait_ge(S["num"], g + 1)
                        if it > 0:
                            act.wait_ge(S["mt"], g)
                        a.activation(NUMS[:].rearrange("p j n -> p (j n)"), bank(4, 2), ACT.Copy).then_inc(S["num_sb"], 1)
                    if it >= 2:
                        for n, t in blocks(it - 2):
                            j = t % 2
                            act.wait_ge(S["qp"], NQ * b + n + 1)
                            if n >= 2:
                                act.wait_ge(S["q_lo"], NQ * b + n - 1)
                            if n >= 3:
                                act.wait_ge(*stored(b, n - 3))
                            if t >= 2:
                                kw = dict(bias=QBS[:, j:j + 1], scale=SCALE)
                            else:
                                kw = dict(bias=COLS[:, 3, j:j + 1])
                            a.activation(TMP[:, n % 2], bank(2 + n % 2), ACT.Identity, **kw).then_inc(S["q_tmp"], 1)
                            a.activation(QKS[:, n % 3, 0], bank(2 + n % 2), ACT.Identity, **kw).then_inc(S["q_hi"], 1)
                    if 1 <= it <= NC:
                        act.wait_ge(S["x2T"], b * NC + it)
                        for k in range(KD):
                            a.activation(XNT[:, k], bank(k), ACT.Identity, bias=COLS[:, 1, k:k + 1],
                                         scale=COLS[:, 0, k:k + 1]).then_inc(S["xn_sb"], 1)
                for u in range(NU):
                    n0 = (NU * b + u) * STEPS
                    for s in range(STEPS):
                        act.wait_ge(S["sc_b"], n0 + s + 1)
                        a.activation(PR[:, s % 2].rearrange("p a n -> p (a n)"), bank(2 + s % 2 * 2, 2),
                                     ACT.Exp).then_inc(S["ex"], 1)
                    act.wait_ge(S["cps"], NU * b + u + 1)
                    if u >= 2:
                        act.wait_ge(S["c_out"], NU * b + u - 1)
                    a.activation(CS[:, u % 2], PS[2 * DH:4 * DH, 6 + u % 2, :], ACT.Copy).then_inc(S["cs_up"], 1)

        def finish(dve, v, b, u):
            h, c = units[u]
            z = NC if h >= 4 else c
            r = h % 4 * DH
            dve.wait_ge(S["cs_up"], NU * b + u + 1)
            v.tensor_tensor(NUM[r:r + DH, z], PS[0:DH, 6 + u % 2, :], CS[0:DH, u % 2], ALU.add).then_inc(S["fin_n"], 1)
            v.tensor_tensor(SUM[r:r + DH, z], PS[DH:2 * DH, 6 + u % 2, :], CS[DH:2 * DH, u % 2], ALU.add
                            ).then_inc(S["c_out"], 1)

        @block.vector
        def _(dve):
            v = nc.vector
            own = Chain(dve, S["dve_own"])
            dve.wait_ge(S["sig"], 1)
            own(v.tensor_scalar_add(CE[:], CE[:], 1.0))
            own(v.reciprocal(SC[:], CE[:]))
            own(v.tensor_tensor(SC[:], SC[:], CT[:], ALU.mult))
            for k in range(KD):
                for b in range(B):
                    v.tensor_copy(SCB[:, k, b], SC[:, k, b:b + 1].broadcast_to([P, P])).then_inc(S["sc_ok"], 1)
            dests = [(W1T, 0, QS), (W1T, 1, QS), (W1T, 2, 1.0), (WoT, 0, 1.0),
                     (W2T, 0, 1.0), (W2T, 1, 1.0), (W2T, 2, 1.0), (OWT, 0, 1.0)]
            for w, (dst, o, s) in enumerate(dests):
                dve.wait_ge(S["wT"], w + 1)
                v.tensor_scalar(dst[:, :, o * D:(o + 1) * D], bank(w).rearrange("p (k n) -> p k n", k=KD), s, None,
                                ALU.mult).then_inc(S["wT_sb"], 1)
            for j in range(2):
                dve.wait_ge(S["pT"], j + 1)
                v.tensor_copy(PB[:, j], bank(j)).then_inc(S["pT_sb"], 1)
            dve.wait_ge(S["wT_sb"], 8)
            dve.wait_ge(S["mk0"], 2)
            for e in (2, 3):
                m = width[e]
                own(v.tensor_copy(W2M[0:m, e - 2], W2T[0:m, 0]))
                own(v.tensor_copy(OWM[0:m, e - 2, 0:m], OWT[0:m, 0, 0:m]))
            dve.wait_ge(S["vec_in"], 16 * 7)
            own(v.tensor_scalar(QBS[:], COLS[:, 2], SCALE, None, ALU.mult))
            dve.wait_ge(S["mod"], 1)
            fm = bank(2)[:, 0:2 * KD * B].rearrange("p (m k b) -> p m k b", m=2, k=KD)
            own(v.tensor_copy(MODC[:, 0], fm[:, 0]))
            own(v.tensor_scalar(MODC[:, 1], fm[:, 1], 1.0, None, ALU.add))
            for b in range(B):
                dve.wait_ge(S["mod"], b + 2)
                own(v.tensor_copy(MODB[:, b].rearrange("p m d -> p (m d)"), bank(4 + b % 2 * 2, 2)))
                v.tensor_scalar(MODB[:, b, 2], MODB[:, b, 2], 1.0, None, ALU.add).then_inc(S["mod_sb"], 1)
            for m, z in ((0, 0), (3, 1)):
                gate = MODB[:, :, m]
                t0, t1 = GS[:, :, 0], GS[:, :, 1]
                own(v.tensor_scalar(t0, gate, 0.0, 2.0, ALU.is_ge, ALU.mult))
                own(v.tensor_scalar(t0, t0, -1.0, None, ALU.add))
                own(v.scalar_tensor_tensor(t1, gate, -1.0, gate, ALU.mult, ALU.max))
                own(v.scalar_tensor_tensor(gate, t1, FLOOR, t0, ALU.max, ALU.mult))
            dve.wait_ge(S["mod_sb"], B)
            v.tensor_copy(VE[:, 0:1], QBS[:, 0:1]).then_inc(S["setup_ok"], 1)
            dve.wait_ge(S["setup_ok"], 1)

            def statistics(tiles, srcs, signal):
                for t, src in zip(tiles, srcs):
                    v.bn_stats(STAT[:, t], src).then_inc(S["dve_own"], 1)
                    own.n += 1
                wait_apart(dve, (S["dve_own"], own.base + own.n))
                for t in tiles:
                    v.bn_aggr(MV[:, t], STAT[:, t]).then_inc(S["dve_own"], 1)
                    own.n += 1
                dve.wait_ge(S["dve_own"], own.base + own.n)
                sl = slice(tiles[0], tiles[-1] + 1)
                v.tensor_scalar(VE[:, sl], MV[:, sl, 1], NORM_EPS, None, ALU.add).then_inc(S[signal], 1)

            def centred(dst, src, t):
                return v.tensor_scalar(dst, src, MV[:, t, 0:1], RSTD[:, t:t + 1], ALU.subtract, ALU.mult)

            def token_tile(s, i):
                return X[:, bass.ds(s * TPC + i, 1)].rearrange("p t d -> p (t d)")

            with dve.Fori(0, B) as b:
                own.enter(b, PER_B)
                own(v.memset(KVS[:], 0.0))
                own(v.memset(NW[:], 0.0))
                own(v.memset(DW[:], 0.0))

                def first_stats(s):
                    statistics(range(TPC), [token_tile(s, i) for i in range(TPC)], "ve1")

                def first_norm(s):
                    g = b * NC + s
                    wait_apart(dve, (S["rstd1"], g + 1))
                    dve.wait_ge(S["xT"], 1 + g)
                    for i in range(TPC):
                        centred(XH[:, i], token_tile(s, i), i).then_inc(S["xh"], 1)

                def chunk(s, last):
                    g = b * NC + s
                    t0 = g * TPC
                    dve.wait_ge(S["v1_ones"], b + 1)
                    for i in range(TPC):
                        dve.wait_ge(S["qkv"], t0 + i + 1)
                        v.tensor_copy(V1[:, i, :, 0:DK], bank(3 + i % 2 * 2)[:, 0:D].rearrange("p (h d) -> p h d", h=NH)
                                      ).then_inc(S["v_sb"], 1)
                        dve.wait_ge(S["sq"], t0 + i + 1)
                        v.tensor_reduce(N2[:, i], SQ[:, i % 2].rearrange("p (h d) -> p h d", d=DK), AX.X, ALU.add
                                        ).then_inc(S["n2"], 1)

                    def shifted(i, src, mx, dst, n2, ready, read_by, signal):
                        dve.wait_ge(ready, t0 + i + 1)
                        sc = src.rearrange("p (h m) -> p h m", m=NM)
                        own(v.tensor_reduce(mx[:], sc, AX.X, ALU.max))
                        dve.wait_ge(S["n2"], 1 + t0 + i + 1)
                        own(v.scalar_tensor_tensor(mx[:], n2, 0.5, mx[:], ALU.mult, ALU.add))
                        dve.wait_ge(read_by, 1 + t0 + i)
                        v.tensor_tensor(dst[:].rearrange("p (h m) -> p h m", m=NM), sc,
                                        mx[:].rearrange("p (h o) -> p h o", o=1).broadcast_to([P, NH, NM]),
                                        ALU.subtract).then_inc(signal, 1)

                    for i in range(TPC):
                        shifted(i, bank(0, 2), MXK, XSK, N2[:, i, NH:], S["xwk"], S["phik"], S["xk_sb"])
                        shifted(i, bank(2, 2), MXQ, XSQ, N2[:, i, :NH], S["xwq"], S["eqt"], S["xq_sb"])
                        if i == 1 and not last:
                            dve.wait_ge(S["x_rest"], 16 * (NC - 1) * (b + 1))
                            first_stats(s + 1)
                        if i == 2 and not last:
                            first_norm(s + 1)
                    dve.wait_ge(S["kv"], 1 + t0 + TPC)
                    v.tensor_tensor(KVS[:], bank(7)[:, 0:GR * 2 * EV].rearrange("p (g n) -> p g n", g=GR), KVS[:],
                                    ALU.add).then_inc(S["kv_sb"], 1)
                    dve.wait_ge(S["kv_sb"], 1 + g + 1)

                dve.wait_ge(S["x_first"], 16 * (b + 1))
                first_stats(0)
                first_norm(0)
                with dve.Fori(0, NC - 1) as s:
                    own.enter(s, PER_C)
                    chunk(s, False)
                    own.leave(NC - 1)
                chunk(NC - 1, True)
                for half, r in ((0, slice(0, NM)), (1, slice(NM, P))):
                    v.tensor_copy(NW[r, :, half * DK:(half + 1) * DK], KVS[r, :, half * EV:half * EV + DK]
                                  ).then_inc(S["kw_ok"], 1)
                    for j in range(2):
                        c = 2 * j + half
                        v.tensor_copy(DW[r, 4 * j:4 * j + 4, c:c + 1], KVS[r, 4 * j:4 * j + 4, half * EV + DK:half * EV + EV]
                                      ).then_inc(S["kw_ok"], 1)
                own(v.memset(MXN[:], 0.0))

                for it in range(NC + 2):
                    g = b * NC + it
                    if it < NC:
                        dve.wait_ge(S["denT"], g + 1)
                        own(v.tensor_scalar(R[:], bank(7).rearrange("p (i q n) -> p i q n", i=TPC, q=4)[:, :, :, 0:4],
                                            FAVOR_EPS, None, ALU.add))
                        own(v.reciprocal(R[:], R[:]))
                        for j in range(2):
                            rj = R[:].rearrange("p i q n -> p (i q) n")[:, :, 2 * j:2 * j + 2]
                            v.tensor_copy(RB[:, j].rearrange("p i (q h d) -> p (i q) h d", q=4, h=2),
                                          rj.rearrange("p a (h o) -> p a h o", o=1).broadcast_to([P, TPC * 4, 2, DK])
                                          ).then_inc(S["rb"], 1)
                    if it >= 2:
                        for n, t in blocks(it - 2):
                            dve.wait_ge(S["q_hi"], NQ * b + n + 1)
                            v.tensor_tensor(QKS[:, n % 3, 1], TMP[:, n % 2], QKS[:, n % 3, 0].bitcast(F32),
                                            ALU.subtract).then_inc(S["q_lo"], 1)
                    if it < NC:
                        dve.wait_ge(S["rT"], g + 1)
                        if it > 0:
                            dve.wait_ge(S["yps"], g)
                        v.tensor_tensor(MT[:].rearrange("p j n -> p (j n)"), bank(4, 2),
                                        NUMS[:].rearrange("p j n -> p (j n)"), ALU.mult).then_inc(S["mt"], 1)
                    if it >= 2:
                        for i in range(TPC):
                            n = NT * b + (it - 2) * TPC + i
                            dve.wait_ge(S["vp"], n + 1)
                            v.tensor_tensor(V2[:, expert[it - 2] * TPC + i], bank(i % 2)[:, 0:D], VB[:], ALU.add
                                            ).then_inc(S["v2_sb"], 1)
                    if it < NC:
                        dve.wait_ge(S["yps"], g + 1)
                        if it == 0:
                            dve.wait_ge(S["xb"], NC * (b + 1))
                        v.tensor_tensor(X[:, slot(it)], bank(6, 2).rearrange("p (t d) -> p t d", t=TPC), X[:, slot(it)],
                                        ALU.add).then_inc(S["x1"], 1)
                        dve.wait_ge(S["x1"], g + 1)
                        statistics(range(it * TPC, (it + 1) * TPC), [X[:, it * TPC + i] for i in range(TPC)], "ve2")
                    if 1 <= it <= NC:
                        dve.wait_ge(S["h2"], g)
                        statistics(range((it - 1) * TPC, it * TPC), [Hh[:, (it - 1) * TPC + i] for i in range(TPC)], "ve3")
                    if it < NC:
                        dve.wait_ge(S["rstd2"], g + 1)
                        for i in range(TPC):
                            t = it * TPC + i
                            v_ins = centred(Hh[:, t], X[:, t], t)
                            if i < TPC - 1:
                                own(v_ins)
                        v_ins.then_inc(S["h2a"], 1)
                    if 1 <= it <= NC:
                        dve.wait_ge(S["rstd3"], g)
                        if it > 1:
                            dve.wait_ge(S["x2T"], g - 1)
                        for i in range(TPC):
                            t = (it - 1) * TPC + i
                            centred(X2[:, i], Hh[:, t], t).then_inc(S["x2"], 1)

                own(v.memset(NUM[2 * DH:, 2:4], 0.0))
                own(v.memset(NUM[DH:2 * DH, 3], 0.0))
                own(v.memset(SUM[2 * DH:, 2:4], 1.0))
                own(v.memset(SUM[DH:2 * DH, 3], 1.0))

                def maxima(p0, p1):
                    for p in range(p0, min(p1, NU * MAXU)):
                        u, m = divmod(p, MAXU)
                        dve.wait_ge(S["am"], NU * MAXU * b + p + 1)
                        v.tensor_reduce(MXP[:, u % 2, m // NC, m % NC:m % NC + 1], bank(m % 2), AX.X, ALU.max
                                        ).then_inc(S["am_rd"], 1)
                        if m == MAXU - 1:
                            dve.wait_ge(S["am_rd"], NU * MAXU * b + p + 1)
                            own(v.tensor_reduce(MXN[:, u % 2, 0:TPC], MXP[:, u % 2], AX.X, ALU.max, negate=True))
                            if u >= 2:
                                dve.wait_ge(shift[(u - 2) % 4], 64 * (SHN[(u - 2) % 4] * b + (u - 2) // 4 + 1))
                            v.transpose(MXT[:, u % 2], MXN[:, u % 2]).then_inc(S["mxt"], 1)

                def divide_part(z, q):
                    part = SUM[:, z, q * P:(q + 1) * P]
                    return v.reciprocal(part, part)

                def result(s):
                    e = expert[s]
                    m = width[e]
                    src = out_ps(e).rearrange("p (t d) -> p t d", t=TPC)
                    dve.wait_ge(S["ops"], b * NC + s + 1)
                    dve.wait_ge(S["base"], b * NC + s + 1)
                    v.tensor_tensor(X[:, slot(s), 0:m], src, X[:, slot(s), 0:m], ALU.add).then_inc(S["fin"], 1)

                maxima(0, LOOK)
                for u, (h, c) in enumerate(units):
                    for s in range(STEPS):
                        p = u * MAXU + s * 2 + LOOK
                        maxima(p, p + 2)
                        if s == 1 and u > 0:
                            finish(dve, v, b, u - 1)
                        for z, at in RECIPROCALS:
                            if u == at and s >= 4:
                                if s == 4:
                                    dve.wait_ge(S["c_out"], NU * b + u)
                                divide_part(z, s - 4).then_inc(S["rcp"], 1)
                        if u == NU - 1 and s in OUT_STEPS:
                            result(OUT_STEPS.index(s))
                finish(dve, v, b, NU - 1)
                dve.wait_ge(S["c_out"], NU * (b + 1))
                dve.wait_ge(S["fin_n"], NU * (b + 1))
                for q in range(TPC):
                    own(divide_part(NC, q))
                    part = slice(q * P, (q + 1) * P)
                    v.tensor_tensor(NUM[:, NC, part], NUM[:, NC, part], SUM[:, NC, part], ALU.mult
                                    ).then_inc(S["at_last"], 1)
                result(NC - 1)
                wait_apart(dve, (S["fin"], NC * (b + 1)))
                own.leave(B)

        @block.tensor
        def _(pe):
            mm, tr = nc.tensor.matmul, nc.tensor.transpose
            pe.wait_ge(S["id_ok"], 1)
            pe.wait_ge(S["w_in"], 16 * 8)
            for w in range(8):
                for k in range(KD):
                    for e in range(KD):
                        last = tr(bank(w)[:, k * D + e * P:k * D + (e + 1) * P], WN[:, w, e, k * P:(k + 1) * P], ident[:])
                last.then_inc(S["wT"], 1)
            pe.wait_ge(S["pj_in"], 16 * NH)
            for j in range(2):
                pe.wait_ge(S["wT_sb"], j + 1)
                for q in range(4):
                    last = tr(bank(j)[:, q * P:(q + 1) * P], PN[:, 4 * j + q], ident[:])
                last.then_inc(S["pT"], 1)
            pe.wait_ge(S["c_in"], 16 * (1 + KD))
            pe.wait_ge(S["sc_ok"], KD * B)
            pe.wait_ge(S["wT_sb"], 3)
            for m in range(2):
                for e in range(KD):
                    o = (m * KD + e) * B
                    for k in range(KD):
                        last = mm(bank(2)[:, o:o + B], WM[:, k, m * D + e * P:m * D + (e + 1) * P], SC[:, k],
                                  start=k == 0, stop=k == KD - 1)
            last.then_inc(S["mod"], 1)
            for b in range(B):
                pe.wait_ge(S["wT_sb"], 8)
                if b >= 2:
                    pe.wait_ge(S["mod_sb"], b - 1)
                for q in range(2):
                    for k in range(KD):
                        last = mm(bank(4 + b % 2 * 2 + q), SCB[:, k, b], WM[:, k, (q + 1) * CH:(q + 2) * CH],
                                  start=k == 0, stop=k == KD - 1)
                last.then_inc(S["mod"], 1)
            pe.wait_ge(S["setup_ok"], 1)

            with pe.Fori(0, B) as b:
                def x_transposes(g, free):
                    pe.wait_ge(S["xh"], (g + 1) * TPC)
                    pe.wait_ge(S["xk_sb"], free)
                    for i in range(TPC):
                        for k in range(KD):
                            last = tr(bank(k)[:, i * P:(i + 1) * P], XH[:, i, k * P:(k + 1) * P], ident[:])
                    last.then_inc(S["xT"], 1)

                def chunk(s, last_chunk):
                    g = b * NC + s
                    t0 = g * TPC
                    pe.wait_ge(S["hT"], KD * (g + 1))

                    def qkt(i):
                        pe.wait_ge(S["qk_sb"], t0 + i + 1)
                        pe.wait_ge(S["qkT_sb"], 1 + t0 + i)
                        for q in range(4):
                            last = tr(bank(6)[:, q * P:(q + 1) * P], QK[:, i % 2, q * P:(q + 1) * P], ident[:])
                        last.then_inc(S["qkT"], 1)

                    for i in range(TPC):
                        if i == 0:
                            pe.wait_ge(S["xq_sb"], 1 + t0)
                        elif i == 1:
                            pe.wait_ge(S["phiq"], 1 + t0)
                        else:
                            pe.wait_ge(S["sq"], t0 + i - 1)
                            pe.wait_ge(S["v_sb"], t0 + i - 1)
                        tok = slice(i * P, (i + 1) * P)
                        for k in range(KD):
                            mm(bank(2 + i % 2 * 2), HT[:, k, tok], W1T[:, k, 0:2 * D], start=k == 0, stop=k == KD - 1)
                        for k in range(KD):
                            last = mm(bank(3 + i % 2 * 2)[:, 0:D], HT[:, k, tok], W1T[:, k, 2 * D:],
                                      start=k == 0, stop=k == KD - 1)
                        last.then_inc(S["qkv"], 1)
                        if i >= 1:
                            qkt(i - 1)
                    qkt(TPC - 1)

                    def key_values(i):
                        pe.wait_ge(S["phik"], 1 + t0 + i + 1)
                        pe.wait_ge(S["v_sb"], t0 + i + 1)
                        if i == 0:
                            pe.wait_ge(S["kv_sb"], 1 + g)
                        for q in range(GR):
                            last = mm(bank(7)[:, q * 2 * EV:(q + 1) * 2 * EV], PK[:, i % 2, q * P:(q + 1) * P],
                                      V1[:, i, 2 * q:2 * q + 2, :].rearrange("p h d -> p (h d)"),
                                      start=i == 0 and q == 0, stop=i == TPC - 1, skip_group_check=True)
                        last.then_inc(S["kv"], 1)

                    def query_transposes(i):
                        pe.wait_ge(S["expq"], t0 + i + 1)
                        if i == 0:
                            pe.wait_ge(S["sq"], t0 + TPC)
                            pe.wait_ge(S["v_sb"], t0 + TPC)
                        else:
                            pe.wait_ge(S["phiq"], 1 + t0 + i)
                        for q in range(GR):
                            last = tr(bank(4, 2)[:, q * P:(q + 1) * P], XSQ[:, q * P:(q + 1) * P], ident[:])
                        last.then_inc(S["eqt"], 1)

                    for i in range(TPC):
                        pe.wait_ge(S["qkT_sb"], 1 + t0 + i + 1)
                        for base, o, ready, free in ((0, 2, "xwk", "xk_sb"), (2, 0, "xwq", "xq_sb")):
                            if i > 0:
                                pe.wait_ge(S[free], 1 + t0 + i)
                            elif base == 2:
                                pe.wait_ge(S["sq"], t0 + TPC - 1)
                                pe.wait_ge(S["v_sb"], t0 + TPC - 1)
                            for j in range(2):
                                last = mm(bank(base + j), QKT[:, i, o + j], PB[:, j], start=True, stop=True)
                            last.then_inc(S[ready], 1)
                        if i >= 1:
                            key_values(i - 1)
                            query_transposes(i - 1)
                    if not last_chunk:
                        x_transposes(g + 1, 1 + t0 + TPC)
                    key_values(TPC - 1)
                    query_transposes(TPC - 1)

                x_transposes(b * NC, 1 + b * NT)
                with pe.Fori(0, NC - 1) as s:
                    chunk(s, False)
                chunk(NC - 1, True)
                pe.wait_ge(S["kw_ok"], 6 * (b + 1))
                pe.wait_ge(S["phiq"], 1 + NT * (b + 1))
                pe.wait_ge(S["xq_sb"], 1 + NT * (b + 1))
                pe.wait_ge(S["kv_sb"], 1 + NC * (b + 1))

                for it in range(NC + 2):
                    g = b * NC + it
                    if it < NC:
                        if it > 0:
                            pe.wait_ge(S["x1"], g)
                        for j in range(2):
                            for q in range(4):
                                last = mm(bank(6)[32 * q:32 * q + 32, :], DW[:, 4 * j + q],
                                          PHIQ[:, 4 * j + q, it * CH:(it + 1) * CH], start=j == 0, stop=j == 1,
                                          tile_position=(0, 32 * q))
                        last.then_inc(S["den"], 1)
                        if it > 0:
                            pe.wait_ge(S["mt"], g)
                        for j in range(2):
                            for q in range(4):
                                last = mm(bank(4 + j)[32 * q:32 * q + 32, :], NW[:, 4 * j + q],
                                          PHIQ[:, 4 * j + q, it * CH:(it + 1) * CH], start=True, stop=True,
                                          tile_position=(0, 32 * q))
                        last.then_inc(S["num"], 1)
                        pe.wait_ge(S["den_sb"], g + 1)
                        for i in range(TPC):
                            last = tr(bank(7)[:, i * P:(i + 1) * P], DENS[:, i * P:(i + 1) * P], ident[:])
                        last.then_inc(S["denT"], 1)
                    if it >= 2:
                        s = it - 2
                        e = expert[s]
                        W = W2T if e < 2 else W2M
                        ks = [(k, k) for k in range(KD)] if e == 0 else [(0, 0 if e == 1 else e - 2)]
                        pe.wait_ge(S["xn_sb"], 2 * (b * NC + s + 1))
                        for n, t in blocks(s):
                            j, w = t % 2, (1 if t < 2 else 0)
                            if n >= 2:
                                pe.wait_ge(S["q_hi"], NQ * b + n - 1)
                            for q, (k, wk) in enumerate(ks):
                                last = mm(bank(2 + n % 2), W[:, wk, w * D + j * P:w * D + (j + 1) * P], XNT[:, k],
                                          start=q == 0, stop=q == len(ks) - 1)
                            last.then_inc(S["qp"], 1)
                    if it < NC:
                        pe.wait_ge(S["rb"], 2 * (g + 1))
                        pe.wait_ge(S["num_sb"], g + 1)
                        for j in range(2):
                            for i in range(TPC):
                                last = tr(bank(4 + j)[:, i * P:(i + 1) * P], RB[:, j, i], ident[:])
                        last.then_inc(S["rT"], 1)
                    if it >= 2:
                        for i in range(TPC):
                            n = NT * b + s * TPC + i
                            if i >= 2:
                                pe.wait_ge(S["v2_sb"], n - 1)
                            for q, (k, wk) in enumerate(ks):
                                last = mm(bank(i % 2)[:, 0:D], XNT[:, k, i * P:(i + 1) * P], W[:, wk, 2 * D:],
                                          start=q == 0, stop=q == len(ks) - 1)
                            last.then_inc(S["vp"], 1)
                    if it < NC:
                        pe.wait_ge(S["mt"], g + 1)
                        pe.wait_ge(S["gated"], 2 * (b + 1))
                        for i in range(TPC):
                            for j in range(2):
                                last = mm(bank(6, 2)[:, i * D:(i + 1) * D], MT[:, j, i * P:(i + 1) * P], WoG[:, j],
                                          start=j == 0, stop=j == 1)
                        last.then_inc(S["yps"], 1)
                    if 1 <= it <= NC:
                        pe.wait_ge(S["x2"], g * TPC)
                        if it >= 2:
                            pe.wait_ge(S["v2_sb"], (g - 1) * TPC)
                        for i in range(TPC):
                            for k in range(KD):
                                last = tr(bank(k)[:, i * P:(i + 1) * P], X2[:, i, k * P:(k + 1) * P], ident[:])
                        last.then_inc(S["x2T"], 1)

                pe.wait_ge(S["q_hi"], NQ * (b + 1))
                pe.wait_ge(S["v2_sb"], NT * (b + 1))

                def maxima(p0, p1):
                    for p in range(p0, min(p1, NU * MAXU)):
                        u, m = divmod(p, MAXU)
                        h, c = units[u]
                        ks = heads.index(h) % 4
                        if m == 0:
                            pe.wait_ge(q_in[u % 4], 48 * (SHN[u % 4] * b + u // 4 + 1))
                            pe.wait_ge(k_in[ks], 48 * (2 * b + heads.index(h) // 4 + 1))
                        if p >= 2:
                            pe.wait_ge(S["am_rd"], NU * MAXU * b + p - 1)
                        mm(bank(m % 2), QOP[0:96, u % 4, m // NC * P:(m // NC + 1) * P],
                           KOP[0:96, ks, m % NC * CH:(m % NC + 1) * CH], start=True, stop=True).then_inc(S["am"], 1)

                def output(s):
                    e = expert[s]
                    m = width[e]
                    k = [z for z, _ in RECIPROCALS].index(e)
                    pe.wait_ge(S["at"], len(RECIPROCALS) * b + k + 1)
                    if e == 1:
                        pe.wait_ge(S["am_rd"], NU * MAXU * (b + 1))
                        pe.wait_ge(S["base"], NC * b + 1)
                    if e == 3:
                        pe.wait_ge(S["fin"], NC * b + 2)
                    for i in range(TPC):
                        o = out_ps(e)[:, i * m:(i + 1) * m]
                        last = mm(o, NUM[:, e, i * P:(i + 1) * P],
                                  OWG[:, 0, 0:m] if e == 1 else OWMG[:, e - 2, 0:m], start=True, stop=True)
                    last.then_inc(S["ops"], 1)

                maxima(0, LOOK)
                for u, (h, c) in enumerate(units):
                    n0 = (NU * b + u) * STEPS
                    ks = heads.index(h) % 4
                    pe.wait_ge(shift[u % 4], 64 * (SHN[u % 4] * b + u // 4 + 1))

                    def values(s):
                        pe.wait_ge(S["ex"], n0 + s + 1)
                        if s == 0 and u >= 2:
                            pe.wait_ge(S["c_out"], NU * b + u - 1)
                        for q in range(2):
                            kt = 2 * s + q
                            for z, W in ((0, V2[:, kt, h * DH:(h + 1) * DH]), (1, ones[:])):
                                r = 64 * q + 32 * z
                                last = mm(PS[r:r + DH, 6 + u % 2, :], W, PR[:, s % 2, q], start=s == 0,
                                          stop=s == STEPS - 1, tile_position=(0, r))
                        if s == STEPS - 1:
                            last.then_inc(S["cps"], 1)

                    for s in range(STEPS):
                        for q in range(2):
                            kt = 2 * s + q
                            last = mm(bank(2 + s % 2 * 2 + q), KOP[:, ks, kt * P:(kt + 1) * P], QOP[:, u % 4],
                                      start=True, stop=True)
                        last.then_inc(S["sc_b"], 1)
                        p = u * MAXU + s * 2 + LOOK
                        maxima(p, p + 2)
                        if s > 0:
                            values(s - 1)
                        if u == NU - 1 and s in OUT_STEPS:
                            output(OUT_STEPS.index(s))
                    values(STEPS - 1)
                pe.wait_ge(S["ex"], NU * STEPS * (b + 1))
                pe.wait_ge(S["at"], len(RECIPROCALS) * (b + 1))
                for i in range(TPC):
                    tok = slice(i * P, (i + 1) * P)
                    o = out_ps(0)[:, i * D:(i + 1) * D]
                    mm(o, NUM[:, 0, tok], OWG[:, 0], start=True, stop=False)
                    pe.wait_ge(S["at_last"], TPC * b + i + 1)
                    last = mm(o, NUM[:, NC, tok], OWG[:, 1], start=False, stop=True)
                last.then_inc(S["ops"], 1)


_INS = ['L0_attn_x', 'L0_attn_Wq', 'L0_attn_Wk', 'L0_attn_Wv', 'L0_attn_Wo', 'L0_attn_bo', 'L0_attn_proj',
        'L0_ffn_norm_w', 'L0_ffn_norm_b', 'L0_ffn_q_w', 'L0_ffn_q_b', 'L0_ffn_k_w', 'L0_ffn_k_b',
        'L0_ffn_v_w', 'L0_ffn_v_b', 'L0_ffn_o_w', 'L0_ffn_o_b', 'L0_c', 'L0_wmod']


def kernel(**inputs):
    import numpy as _np
    import concourse.bacc as _bacc
    from concourse import mybir as _mybir
    from concourse.bass_utils import run_bass_kernel_spmd as _run

    nc = _bacc.Bacc("TRN2", target_bir_lowering=False, num_devices=1)
    arrays, args = {}, []
    for name in _INS:
        a = _np.ascontiguousarray(inputs[name])
        arrays[f"in_{name}_dram"] = a
        args.append(nc.dram_tensor(f"in_{name}_dram", a.shape, _mybir.dt.from_np(a.dtype), kind="ExternalInput").ap())
    out = nc.dram_tensor("out_0_dram", inputs['L0_attn_x'].shape, F32, kind="ExternalOutput").ap()
    adaln_block(nc, *args, out)
    r = _run(nc, [arrays], core_ids=[0])
    return r.results[0]["out_0_dram"]
```

```python
from contextlib import ExitStack

import concourse.bass as bass
from concourse import mybir

F32 = mybir.dt.float32
F32R = mybir.dt.float32r
ALU = mybir.AluOpType
ACT = mybir.ActivationFunctionType
AX = mybir.AxisListType

P = 128
CH = 512
TPC = CH // P

FAVOR_EPS = 1e-6
NORM_EPS = 1e-5
FLOOR = 0.25


class Chain:

    def __init__(self, eng, sem, passed=None):
        self.passed = passed
        self.eng, self.sem, self.base, self.n, self.outer = eng, sem, 0, 0, []

    def __call__(self, ins):
        ins.then_inc(self.sem, 1)
        self.n += 1
        self.eng.wait_ge(self.sem, self.base + self.n)
        if self.passed is not None:
            self.eng.sem_inc(self.passed, 1)

    def enter(self, i, per):
        self.outer.append((self.base, self.n, per))
        self.base, self.n = self.base + self.n + i * per, 0

    def leave(self, trips):
        assert self.n == self.outer[-1][2], self.n
        self.base, n, per = self.outer.pop()
        self.n = n + per * trips


def adaln_block(nc, x, Wq, Wk, Wv, Wo, bo, proj, norm_w, norm_b, q_w, q_b, k_w, k_b, v_w, v_b, o_w, o_b,
                cond, wmod, out):
    B, T, D = x.shape
    NH, NM, DK = proj.shape
    H2N, EXPERTS = 8, 4
    DH = D // H2N
    KD = D // P
    NT, NC = T // P, T // CH
    GR = NH * NM // P
    assert NC == EXPERTS and NT == NC * TPC and KD == 2 and GR == 8
    PHI = 1.0 / NM ** 0.5
    QS = 1.0 / DK ** 0.5
    SCALE = float(D) ** -0.5
    width = [D >> e for e in range(EXPERTS)]

    units = [(h, c) for h in range(H2N) for c in range(NC) if h * DH < width[c]]
    NU = len(units)
    KT = T // P
    STEPS = KT // 2
    MAXU = TPC * NC
    loads_of = {}
    for u, (h, c) in enumerate(units):
        loads_of.setdefault(h, u)

    NQ = 3 * NC + 1
    QSN = [len(range(i, NQ, 3)) for i in range(3)]
    SHN = [len(range(i, NU, 4)) for i in range(4)]
    LOOK = MAXU * 3 // 2
    expert = [(s + 1) % NC for s in range(NC)]
    slot_of = {e: s for s, e in enumerate(expert)}
    RECIPROCALS = ((3, 5), (2, 8), (0, 11), (1, 12))
    OUT_STEPS = (2, 4, 6)
    PER_B, PER_C, PER_P = 204, 12, 10


    k_scr = nc.dram_tensor("k_scr", (2, D, T), F32, kind="Internal").ap()
    q_scr = nc.dram_tensor("q_scr", (2, D, T), F32, kind="Internal").ap()

    with ExitStack() as ctx:
        def sb(name, shape, dt=F32, stack=ctx):
            return stack.enter_context(nc.sbuf_tensor(name, shape, dt))

        def sem(name):
            return ctx.enter_context(nc.semaphore(name))

        X = sb("X", [P, NT, D])
        W1T = sb("W1T", [P, KD, 3 * D])
        WoT = sb("WoT", [P, KD, D])
        WoG, BOG = sb("WoG", [P, KD, D]), sb("BOG", [P, D])
        W2T = sb("W2T", [P, KD, 3 * D])
        W2M = sb("W2M", [P, 2, 3 * D])
        OWT = sb("OWT", [P, KD, D])
        OWM = sb("OWM", [P, 2, 64])
        OWG, OWMG = sb("OWG", [P, KD, D]), sb("OWMG", [P, 2, 64])
        PB = sb("PB", [P, 2, CH])
        MODB = sb("MODB", [P, B, 4, D])
        MODC = sb("MODC", [P, 2, KD, B])
        BO, VB, OB = sb("BO", [P, D]), sb("VB", [P, D]), sb("OB", [P, D])
        COLS = sb("COLS", [P, 4, KD])
        QBS = sb("QBS", [P, KD])
        ident = sb("ident", [P, P])
        ones = sb("ones", [P, DH])
        minus_half = sb("minus_half", [P, NT])
        STAT = sb("STAT", [P, NT, 6])
        MV = sb("MV", [P, NT, 2])
        VE = sb("VE", [P, NT])
        RSTD = sb("RSTD", [P, NT])
        KVS = sb("KVS", [P, 2, 2, P])
        NW, DW = sb("NW", [P, GR, 32]), sb("DW", [P, GR, 32])

        s0 = ExitStack()
        WN = sb("WN", [P, 8, KD, D], stack=s0)
        PN = sb("PN", [P, GR, P], stack=s0)
        WM = sb("WM", [P, KD, 6 * D], stack=s0)
        CT = sb("CT", [P, KD, B], stack=s0)
        CE = sb("CE", [P, KD, B], stack=s0)
        SC = sb("SC", [P, KD, B], stack=s0)
        SCB = sb("SCB", [P, KD, B, P], stack=s0)
        GS = sb("GS", [P, B, 2, D], stack=s0)
        s0.close()

        s1 = ExitStack()
        QOP = sb("QOP", [97, 4, CH], F32R, stack=s1)
        KOP = sb("KOP", [97, 4, T], F32R, stack=s1)
        PR = sb("PR", [P, 2, 2, CH], stack=s1)
        CS = sb("CS", [2 * DH, 2, CH], stack=s1)
        SUM = sb("SUM", [P, NC + 1, CH], stack=s1)
        s1.close()
        PHIQ = sb("PHIQ", [P, GR, T])

        s2 = ExitStack()
        XH = sb("XH", [P, 2, D], stack=s2)
        HT = sb("HT", [P, KD, P], stack=s2)
        QK = sb("QK", [P, 2 * D], stack=s2)
        SQ = sb("SQ", [P, 2 * D], stack=s2)
        N2 = sb("N2", [P, 2, 2 * NH], stack=s2)
        QKT = sb("QKT", [P, 4, P], stack=s2)
        MXK, MXQ = sb("MXK", [P, NH], stack=s2), sb("MXQ", [P, NH], stack=s2)
        XSK = sb("XSK", [P, NH * NM], stack=s2)
        XSQ = sb("XSQ", [P, NH * NM], stack=s2)
        PK = sb("PK", [P, 2, NH * NM], stack=s2)
        V1 = sb("V1", [P, 2, D], stack=s2)
        STAT1, MV1 = sb("STAT1", [P, 2, 6], stack=s2), sb("MV1", [P, 2, 2], stack=s2)
        VE1, RSTD1 = sb("VE1", [P, 2], stack=s2), sb("RSTD1", [P, 2], stack=s2)
        s2.close()

        V2 = sb("V2", [P, KT, D])
        Hh = sb("Hh", [P, NT, D])
        X2 = sb("X2", [P, TPC, D])
        XNT = sb("XNT", [P, KD, CH])
        TMP = sb("TMP", [P, 2, CH])
        QKS = sb("QKS", [P, 3, 2, CH], F32R)
        MXP = sb("MXP", [P, 2, TPC, NC])
        MXN = sb("MXN", [P, 2, 32])
        MXT = sb("MXT", [P, 2, 32])
        s3 = ExitStack()
        NUM = sb("NUM", [P, NC + 1, CH], stack=s3)
        s3.close()
        DENS = sb("DENS", [P, CH])
        NUMS = sb("NUMS", [P, 2, CH])
        R = sb("R", [P, TPC, 4, 4])
        RB = sb("RB", [P, 2, TPC, P])
        MT = sb("MT", [P, 2, CH])

        PS = ctx.enter_context(nc.psum_tensor("PS", [P, 8, CH], F32))

        def bank(i, n=1):
            return PS[:, i:i + n, :].rearrange("p b n -> p (b n)")

        def out_ps(e):
            if e == 0:
                return bank(4, 2)
            return bank(0) if e == 1 else bank(1)[:, (0 if e == 2 else 4 * width[2]):][:, 0:TPC * width[e]]

        names = """w_in c_in vec_in pj_in id0 id_ok nb0 mh_ok mk0
                   wT wT_sb pT pT_sb sig sc_ok mod mod_sb setup_ok
                   x_first x_rest ve1 rstd1 xh xT hT qkv qk_sb sq v_sb n2 qkT qkT_sb xwk xwq xk_sb xq_sb expk expq
                   phik kv kv_sb eqt kvT phiq gated xb kw_ok
                   den den_sb num num_sb denT rb rT mt yps x1
                   ve2 rstd2 ve3 rstd3 h2a h2m h2 x2 x2T xn_sb qp q_tmp q_hi q_lo scr0 scr1 scr2 vp v2_sb init_ok
                   q_in0 q_in1 q_in2 q_in3 k_in0 k_in1 k_in2 k_in3 am am_rd mxt shift0 shift1 shift2 shift3
                   sc_b ex cps cs_up c_out pool_own rcp at at_last base ops fin st0 st1 st2 st3 fin_n dve_own passed""".split()
        S = {n: sem(n) for n in names}
        q_in = [S[f"q_in{i}"] for i in range(4)]
        k_in = [S[f"k_in{i}"] for i in range(4)]
        shift = [S[f"shift{i}"] for i in range(4)]

        block = ctx.enter_context(nc.Block())
        xv = x.rearrange("b (c t p) d -> p (b c) t d", p=P, t=TPC)
        ov = out.rearrange("b (c t p) d -> p (b c) t d", p=P, t=TPC)
        heads = sorted(loads_of)
        last_unit = {h: max(u for u, (hh, _) in enumerate(units) if hh == h) for h in heads}
        scr = [S[f"scr{i}"] for i in range(3)]
        st = [S[f"st{i}"] for i in range(NC)]

        def slot(s):
            return slice(s * TPC, (s + 1) * TPC)

        def blocks(s):
            return [(3 * s + t, t) for t in ((0, 1, 2, 3) if expert[s] == 0 else (0, 1, 2))]

        def stored(b, n):
            return scr[n % 3], 32 * (QSN[n % 3] * b + n // 3 + 1)

        def over_tiles(eng, tile, own=None):
            for t in range(2):
                tile(t, t, t)
            with eng.Fori(0, NT // 2 - 3) as i:
                if own is not None:
                    own.enter(i, PER_C)
                for par in range(2):
                    tile(i * 2 + 2 + par, par, NT // 2)
                if own is not None:
                    own.leave(NT // 2 - 3)
            for t in range(NT - 4, NT):
                tile(t, t % 2, t)

        def wait_apart(eng, *waits):
            for s_, value in waits:
                eng.wait_ge(s_, value)
                eng.sem_inc(S["passed"], 1)

        @block.sync
        def _(sp):
            for w, src in enumerate((Wq, Wk, Wv, Wo, q_w, k_w, v_w, o_w)):
                sp.dma_start(WN[:, w], src.rearrange("(e p) d -> p e d", p=P)).then_inc(S["w_in"], 16)
            sp.dma_start(WM[:], wmod.rearrange("(k p) n -> p k n", p=P)).then_inc(S["c_in"], 16)
            for k in range(KD):
                sp.dma_start(CT[:, k], cond[:, k * P:(k + 1) * P].rearrange("b p -> p b"),
                             allow_slow_non_contiguous=True).then_inc(S["c_in"], 16)
            for dst, src in ((BO, bo), (VB, v_b), (OB, o_b)):
                sp.dma_start(dst[:], src.rearrange("(a n) -> a n", a=1).broadcast_to([P, D])).then_inc(S["vec_in"], 16)
            for n, src in enumerate((norm_w, norm_b, q_b, k_b)):
                sp.dma_start(COLS[:, n], src.rearrange("(k p) -> p k", p=P),
                             allow_slow_non_contiguous=True).then_inc(S["vec_in"], 16)
            sp.wait_ge(S["nb0"], 1)
            for h in range(NH):
                r, c = h % 2 * NM, h % 8 * DK
                sp.dma_start(PN[r:r + NM, h // 2, c:c + DK], proj[h]).then_inc(S["pj_in"], 16)

            def load_x(b, s):
                sp.dma_start(X[:, slot(s)], xv[:, bass.ds(b * NC + expert[s], 1)].rearrange("p o t d -> p (o t) d")
                             ).then_inc(S["x_first" if s == 0 else "x_rest"], 16)

            for s in range(NC):
                load_x(0, s)

            def batch(b, last):
                for s in range(NC):
                    e = expert[s]
                    for n, t in blocks(s):
                        dst, j = (k_scr, t) if t < 2 else (q_scr, t - 2)
                        sp.wait_ge(S["q_lo"], NQ * b + n + 1)
                        for half in range(2):
                            sp.dma_start(dst[half, j * P:(j + 1) * P, e * CH:(e + 1) * CH],
                                         QKS[:, n % 3, half].bitcast(F32)).then_inc(scr[n % 3], 16)

                def load_k(h):
                    s = heads.index(h) % 4
                    for r, half in ((0, 0), (32, 0), (64, 1)):
                        sp.dma_start(KOP[r:r + DH, s].bitcast(F32),
                                     k_scr[half, h * DH:(h + 1) * DH, :]).then_inc(k_in[s], 16)

                def load_q(u):
                    h, c = units[u]
                    for r, half in ((0, 0), (32, 1), (64, 0)):
                        sp.dma_start(QOP[r:r + DH, u % 4].bitcast(F32),
                                     q_scr[half, h * DH:(h + 1) * DH, c * CH:(c + 1) * CH]).then_inc(q_in[u % 4], 16)

                def load_shift(u):
                    sp.wait_ge(S["mxt"], NU * b + u + 1)
                    for g in range(4):
                        dst = QOP[96:97, u % 4, :].bitcast(F32).rearrange("o (t g n) -> o t g n", t=TPC, g=4)[:, :, g]
                        sp.dma_start(dst, MXT[32 * g:32 * g + TPC, u % 2, :]).then_inc(shift[u % 4], 16)

                wait_apart(sp, *[stored(b, n) for n in range(NQ - 3, NQ)], (S["init_ok"], b + 1))
                loaded_k = set()
                for u in range(4):
                    h = units[u][0]
                    if h not in loaded_k:
                        load_k(h)
                        loaded_k.add(h)
                    load_q(u)
                for h in heads[1:4]:
                    if h not in loaded_k:
                        load_k(h)
                        loaded_k.add(h)
                load_shift(0)
                for u in range(NU):
                    if u + 1 < NU:
                        load_shift(u + 1)
                    if u < NU - 1:
                        wait_apart(sp, (S["sc_b"], STEPS * (NU * b + u + 1)))
                    if u + 4 < NU:
                        load_q(u + 4)
                    for h in heads[4:]:
                        if h not in loaded_k and last_unit[heads[heads.index(h) - 4]] <= u:
                            load_k(h)
                            loaded_k.add(h)
                for s in range(NC):
                    sp.wait_ge(S["fin"], NC * b + s + 1)
                    sp.dma_start(ov[:, bass.ds(b * NC + expert[s], 1)].rearrange("p o t d -> p (o t) d"),
                                 X[:, slot(s)]).then_inc(st[s], 16)
                    if s > 0 and not last:
                        wait_apart(sp, (st[s - 1], 16 * (b + 1)))
                        load_x(b + 1, s - 1)
                if not last:
                    wait_apart(sp, (st[NC - 1], 16 * (b + 1)))
                    load_x(b + 1, NC - 1)

            with sp.Fori(0, B - 1) as b:
                batch(b, False)
            batch(B - 1, True)
            for s in range(NC):
                sp.wait_ge(st[s], 16 * B)

        @block.gpsimd
        def _(pool):
            g = nc.gpsimd
            g.memset(PN[:], 0.0).then_inc(S["nb0"], 1)
            g.memset(ident[:], 0.0).then_inc(S["id0"], 1)
            pool.wait_ge(S["id0"], 1)
            g.affine_select(out=ident[:], in_=ident[:], compare_op=ALU.not_equal, fill=1.0, base=0,
                            pattern=[[-1, P]], channel_multiplier=1).then_inc(S["id_ok"], 1)
            g.memset(minus_half[:], -0.5).then_inc(S["mh_ok"], 1)
            g.memset(ones[:], 1.0).then_inc(S["mh_ok"], 1)
            g.memset(W2M[:], 0.0).then_inc(S["mk0"], 1)
            g.memset(OWM[:], 0.0).then_inc(S["mk0"], 1)
            pool.wait_ge(S["mh_ok"], 2)
            pool.wait_ge(S["setup_ok"], 1)
            with pool.Fori(0, B) as b:
                def rsqrt(cols, ready, signal, n):
                    wait_apart(pool, (S[ready], n))
                    g.tensor_tensor(RSTD[:, cols], VE[:, cols], minus_half[:, cols], ALU.pow).then_inc(S[signal], 1)

                def rsqrt_tile(t, par):
                    wait_apart(pool, (S["ve1"], b * NT + t + 1))
                    g.tensor_tensor(RSTD1[:, par:par + 1], VE1[:, par:par + 1], minus_half[:, 0:1], ALU.pow
                                    ).then_inc(S["rstd1"], 1)

                rsqrt_tile(0, 0)
                gate = MODB[:, bass.ds(b, 1), 0, :]
                g.tensor_tensor(WoG[:], WoT[:], gate.broadcast_to([P, KD, D]), ALU.mult).then_inc(S["gated"], 1)
                g.tensor_tensor(BOG[:], BO[:], gate.rearrange("p o d -> p (o d)"), ALU.mult).then_inc(S["gated"], 1)

                rsqrt_tile(1, 1)
                rsqrt_tile(2, 0)

                def tile(t, par, at):
                    n = b * NT + t
                    if at >= 2:
                        wait_apart(pool, (S["kv"], n - 1))
                    wait_apart(pool, (S["expk"], n + 1))
                    g.tensor_scalar(PK[:, par], XSK[:], FAVOR_EPS, PHI, ALU.add, ALU.mult).then_inc(S["phik"], 1)
                    if at < NT - 3:
                        rsqrt_tile(t + 3, 1 - par)
                    wait_apart(pool, (S["xh"], n + 1), (S["gated"], 2 * (b + 1)))
                    src = X[:, bass.ds(t, 1)].rearrange("p t d -> p (t d)")
                    g.tensor_tensor(src, src, BOG[:], ALU.add).then_inc(S["xb"], 1)

                over_tiles(pool, tile)
                for it in range(NC + 1):
                    if it >= 1:
                        s = it - 1
                        for op, m, ready, signal in ((ALU.mult, 2, "h2a", "h2m"), (ALU.add, 1, "h2m", "h2")):
                            wait_apart(pool, (S[ready], NC * b + s + 1))
                            g.tensor_tensor(Hh[:, slot(s)], Hh[:, slot(s)],
                                            MODB[:, bass.ds(b, 1), m, :].broadcast_to([P, TPC, D]), op
                                            ).then_inc(S[signal], 1)
                    if it < NC:
                        rsqrt(slot(it), "ve2", "rstd2", NC * b + it + 1)
                    if it >= 1:
                        rsqrt(slot(it - 1), "ve3", "rstd3", NC * b + it)
                wait_apart(pool, (S["num"], NC * (b + 1)), (S["rstd3"], NC * (b + 1)))
                g.memset(KOP[96:97].bitcast(F32), 1.0).then_inc(S["init_ok"], 1)

                wait_apart(pool, (S["x2"], NT * (b + 1)), (S["init_ok"], b + 1))
                own_g = Chain(pool, S["pool_own"], S["passed"])
                own_g.enter(b, PER_P)
                gate = MODB[:, bass.ds(b, 1), 3, :]
                own_g(g.tensor_tensor(OWG[:], OWT[:], gate.broadcast_to([P, KD, D]), ALU.mult))
                own_g(g.tensor_tensor(OWMG[:], OWM[:], gate[:, :, 0:64].broadcast_to([P, 2, 64]), ALU.mult))
                for s in range(NC):
                    m = width[expert[s]]
                    own_g(g.tensor_tensor(Hh[:, slot(s), 0:m], Hh[:, slot(s), 0:m], OB[:, 0:m]
                                          .rearrange("p (o d) -> p o d", o=1).broadcast_to([P, TPC, m]), ALU.add))
                    own_g(g.tensor_tensor(Hh[:, slot(s)], Hh[:, slot(s)], gate.broadcast_to([P, TPC, D]), ALU.mult))
                    g.tensor_tensor(X[:, slot(s)], X[:, slot(s)], Hh[:, slot(s)], ALU.add).then_inc(S["base"], 1)
                own_g.leave(B)
                for k, (z, _) in enumerate(RECIPROCALS):
                    wait_apart(pool, (S["rcp"], TPC * (len(RECIPROCALS) * b + k + 1)))
                    g.tensor_tensor(NUM[:, z], NUM[:, z], SUM[:, z], ALU.mult).then_inc(S["at"], 1)
        @block.scalar
        def _(act):
            a = nc.scalar
            act.wait_ge(S["c_in"], 16 * (1 + KD))
            a.activation(CE[:], CT[:], ACT.Exp, scale=-1.0).then_inc(S["sig"], 1)
            act.wait_ge(S["setup_ok"], 1)
            with act.Fori(0, B) as b:
                def modulated(t, at):
                    n = b * NT + t
                    waits = [(S["xT"], n + 1)]
                    if at >= 1:
                        waits.append((S["qkv"], n))
                    wait_apart(act, *waits)
                    for k in range(KD):
                        a.activation(HT[:, k], bank(6)[:, D + k * P:D + (k + 1) * P], ACT.Identity,
                                     bias=MODC[:, 0, k, bass.ds(b, 1)], scale=MODC[:, 1, k, bass.ds(b, 1)]
                                     ).then_inc(S["hT"], 1)

                def project(t, at):
                    n = b * NT + t
                    act.wait_ge(S["qkv"], n + 1)
                    if at >= 1:
                        act.wait_ge(S["qkT"], n)
                    a.activation(QK[:], bank(4), ACT.Copy).then_inc(S["qk_sb"], 1)

                def squares(t, at):
                    n = b * NT + t
                    if at >= 1:
                        act.wait_ge(S["n2"], n)
                    a.activation(SQ[:], bank(4), ACT.Square).then_inc(S["sq"], 1)

                def transposed(t):
                    act.wait_ge(S["qkT"], b * NT + t + 1)
                    a.activation(QKT[:].rearrange("p a n -> p (a n)"), bank(4), ACT.Copy).then_inc(S["qkT_sb"], 1)

                def query_features(t, half):
                    wait_apart(act, (S["eqt"], 2 * (b * NT + t) + half + 1))
                    a.activation(PHIQ[:, half * 4:half * 4 + 4, bass.ds(t * P, P)],
                                 bank(5).rearrange("p (g n) -> p g n", g=4), ACT.Copy, bias=FAVOR_EPS * PHI,
                                 scale=PHI).then_inc(S["phiq"], 1)

                modulated(0, 0)
                project(0, 0)
                squares(0, 0)
                transposed(0)
                modulated(1, 1)

                def tile(t, par, at):
                    n = b * NT + t
                    act.wait_ge(S["xk_sb"], n + 1)
                    a.activation(XSK[:], XSK[:], ACT.Exp).then_inc(S["expk"], 1)
                    if at < NT - 1:
                        project(t + 1, at + 1)
                    if at >= 1:
                        query_features(t - 1, 0)
                    if at < NT - 1:
                        squares(t + 1, at + 1)
                    if at >= 1:
                        query_features(t - 1, 1)
                    if at < NT - 1:
                        transposed(t + 1)
                    if at < NT - 2:
                        modulated(t + 2, at + 2)
                    act.wait_ge(S["xq_sb"], n + 1)
                    a.activation(XSQ[:], XSQ[:], ACT.Exp).then_inc(S["expq"], 1)

                over_tiles(act, tile)
                query_features(NT - 1, 0)
                query_features(NT - 1, 1)

                for it in range(NC + 3):
                    if it < NC:
                        g = b * NC + it
                        act.wait_ge(S["den"], g + 1)
                        if it > 0:
                            act.wait_ge(S["denT"], g)
                        a.activation(DENS[:], bank(6), ACT.Copy).then_inc(S["den_sb"], 1)
                        act.wait_ge(S["num"], g + 1)
                        if it > 0:
                            act.wait_ge(S["mt"], g)
                        a.activation(NUMS[:].rearrange("p j n -> p (j n)"), bank(4, 2), ACT.Copy).then_inc(S["num_sb"], 1)
                    if it >= 3:
                        for n, t in blocks(it - 3):
                            j = t % 2
                            act.wait_ge(S["qp"], NQ * b + n + 1)
                            if n >= 2:
                                act.wait_ge(S["q_lo"], NQ * b + n - 1)
                            if n >= 3:
                                act.wait_ge(*stored(b, n - 3))
                            if t >= 2:
                                kw = dict(bias=QBS[:, j:j + 1], scale=SCALE)
                            else:
                                kw = dict(bias=COLS[:, 3, j:j + 1])
                            a.activation(TMP[:, n % 2], bank(2 + n % 2), ACT.Identity, **kw).then_inc(S["q_tmp"], 1)
                            a.activation(QKS[:, n % 3, 0], bank(2 + n % 2), ACT.Identity, **kw).then_inc(S["q_hi"], 1)
                    if 2 <= it < NC + 2:
                        act.wait_ge(S["x2T"], b * NC + it - 1)
                        for k in range(KD):
                            a.activation(XNT[:, k], bank(k), ACT.Identity, bias=COLS[:, 1, k:k + 1],
                                         scale=COLS[:, 0, k:k + 1]).then_inc(S["xn_sb"], 1)
                for u in range(NU):
                    n0 = (NU * b + u) * STEPS
                    for s in range(STEPS):
                        act.wait_ge(S["sc_b"], n0 + s + 1)
                        a.activation(PR[:, s % 2].rearrange("p a n -> p (a n)"), bank(2 + s % 2 * 2, 2),
                                     ACT.Exp).then_inc(S["ex"], 1)
                    act.wait_ge(S["cps"], NU * b + u + 1)
                    if u >= 2:
                        act.wait_ge(S["c_out"], NU * b + u - 1)
                    a.activation(CS[:, u % 2], PS[2 * DH:4 * DH, 6 + u % 2, :], ACT.Copy).then_inc(S["cs_up"], 1)

        def finish(dve, v, b, u):
            h, c = units[u]
            z = NC if h >= 4 else c
            r = h % 4 * DH
            dve.wait_ge(S["cs_up"], NU * b + u + 1)
            v.tensor_tensor(NUM[r:r + DH, z], PS[0:DH, 6 + u % 2, :], CS[0:DH, u % 2], ALU.add).then_inc(S["fin_n"], 1)
            v.tensor_tensor(SUM[r:r + DH, z], PS[DH:2 * DH, 6 + u % 2, :], CS[DH:2 * DH, u % 2], ALU.add
                            ).then_inc(S["c_out"], 1)

        @block.vector
        def _(dve):
            v = nc.vector
            own = Chain(dve, S["dve_own"])
            dve.wait_ge(S["sig"], 1)
            own(v.tensor_scalar_add(CE[:], CE[:], 1.0))
            own(v.reciprocal(SC[:], CE[:]))
            own(v.tensor_tensor(SC[:], SC[:], CT[:], ALU.mult))
            for k in range(KD):
                for b in range(B):
                    v.tensor_copy(SCB[:, k, b], SC[:, k, b:b + 1].broadcast_to([P, P])).then_inc(S["sc_ok"], 1)
            dests = [(W1T, 0, QS), (W1T, 1, QS), (W1T, 2, 1.0), (WoT, 0, 1.0),
                     (W2T, 0, 1.0), (W2T, 1, 1.0), (W2T, 2, 1.0), (OWT, 0, 1.0)]
            for w, (dst, o, s) in enumerate(dests):
                dve.wait_ge(S["wT"], w + 1)
                v.tensor_scalar(dst[:, :, o * D:(o + 1) * D], bank(w).rearrange("p (k n) -> p k n", k=KD), s, None,
                                ALU.mult).then_inc(S["wT_sb"], 1)
            for j in range(2):
                dve.wait_ge(S["pT"], j + 1)
                v.tensor_copy(PB[:, j], bank(j)).then_inc(S["pT_sb"], 1)
            dve.wait_ge(S["wT_sb"], 8)
            dve.wait_ge(S["mk0"], 2)
            for e in (2, 3):
                m = width[e]
                own(v.tensor_copy(W2M[0:m, e - 2], W2T[0:m, 0]))
                own(v.tensor_copy(OWM[0:m, e - 2, 0:m], OWT[0:m, 0, 0:m]))
            dve.wait_ge(S["vec_in"], 16 * 7)
            own(v.tensor_scalar(QBS[:], COLS[:, 2], SCALE, None, ALU.mult))
            dve.wait_ge(S["mod"], 1)
            fm = bank(2)[:, 0:2 * KD * B].rearrange("p (m k b) -> p m k b", m=2, k=KD)
            own(v.tensor_copy(MODC[:, 0], fm[:, 0]))
            own(v.tensor_scalar(MODC[:, 1], fm[:, 1], 1.0, None, ALU.add))
            for b in range(B):
                dve.wait_ge(S["mod"], b + 2)
                own(v.tensor_copy(MODB[:, b].rearrange("p m d -> p (m d)"), bank(4 + b % 2 * 2, 2)))
                v.tensor_scalar(MODB[:, b, 2], MODB[:, b, 2], 1.0, None, ALU.add).then_inc(S["mod_sb"], 1)
            for m, z in ((0, 0), (3, 1)):
                gate = MODB[:, :, m]
                t0, t1 = GS[:, :, 0], GS[:, :, 1]
                own(v.tensor_scalar(t0, gate, 0.0, 2.0, ALU.is_ge, ALU.mult))
                own(v.tensor_scalar(t0, t0, -1.0, None, ALU.add))
                own(v.scalar_tensor_tensor(t1, gate, -1.0, gate, ALU.mult, ALU.max))
                own(v.scalar_tensor_tensor(gate, t1, FLOOR, t0, ALU.max, ALU.mult))
            dve.wait_ge(S["mod_sb"], B)
            v.tensor_copy(VE[:, 0:1], QBS[:, 0:1]).then_inc(S["setup_ok"], 1)
            dve.wait_ge(S["setup_ok"], 1)

            def statistics(tiles, srcs, signal):
                for t, src in zip(tiles, srcs):
                    v.bn_stats(STAT[:, t], src).then_inc(S["dve_own"], 1)
                    own.n += 1
                wait_apart(dve, (S["dve_own"], own.base + own.n))
                for t in tiles:
                    v.bn_aggr(MV[:, t], STAT[:, t]).then_inc(S["dve_own"], 1)
                    own.n += 1
                dve.wait_ge(S["dve_own"], own.base + own.n)
                sl = slice(tiles[0], tiles[-1] + 1)
                v.tensor_scalar(VE[:, sl], MV[:, sl, 1], NORM_EPS, None, ALU.add).then_inc(S[signal], 1)

            def centred(dst, src, t):
                return v.tensor_scalar(dst, src, MV[:, t, 0:1], RSTD[:, t:t + 1], ALU.subtract, ALU.mult)

            own(v.memset(NW[:], 0.0))
            own(v.memset(DW[:], 0.0))
            with dve.Fori(0, B) as b:
                own.enter(b, PER_B)

                def first_statistics(t, par):
                    v.bn_stats(STAT1[:, par], X[:, bass.ds(t, 1)].rearrange("p t d -> p (t d)")
                               ).then_inc(S["dve_own"], 1)
                    own.n += 1
                    wait_apart(dve, (S["dve_own"], own.base + own.n))
                    own(v.bn_aggr(MV1[:, par], STAT1[:, par]))
                    v.tensor_scalar(VE1[:, par:par + 1], MV1[:, par, 1:2], NORM_EPS, None, ALU.add
                                    ).then_inc(S["ve1"], 1)

                def first_norm(t, par, at):
                    n = b * NT + t
                    wait_apart(dve, (S["rstd1"], n + 1))
                    if at >= 2:
                        dve.wait_ge(S["xT"], n - 1)
                    v.tensor_scalar(XH[:, par], X[:, bass.ds(t, 1)].rearrange("p t d -> p (t d)"), MV1[:, par, 0:1],
                                    RSTD1[:, par:par + 1], ALU.subtract, ALU.mult).then_inc(S["xh"], 1)

                def values_out(t, par, at):
                    n = b * NT + t
                    dve.wait_ge(S["qkv"], n + 1)
                    if at >= 2:
                        dve.wait_ge(S["kv"], n - 1)
                    v.tensor_copy(V1[:, par], bank(6)[:, 0:D]).then_inc(S["v_sb"], 1)

                def norms(t, par):
                    dve.wait_ge(S["sq"], b * NT + t + 1)
                    v.tensor_reduce(N2[:, par], SQ[:].rearrange("p (h d) -> p h d", d=DK), AX.X, ALU.add
                                    ).then_inc(S["n2"], 1)

                def shifted(n, at, src, mx, dst, n2, ready, read_by, read_count, signal):
                    dve.wait_ge(ready, n + 1)
                    sc = src.rearrange("p (h m) -> p h m", m=NM)
                    own(v.tensor_reduce(mx[:], sc, AX.X, ALU.max))
                    dve.wait_ge(S["n2"], n + 1)
                    own(v.scalar_tensor_tensor(mx[:], n2, 0.5, mx[:], ALU.mult, ALU.add))
                    if at >= 1:
                        dve.wait_ge(read_by, read_count)
                    v.tensor_tensor(dst[:].rearrange("p (h m) -> p h m", m=NM), sc,
                                    mx[:].rearrange("p (h o) -> p h o", o=1).broadcast_to([P, NH, NM]),
                                    ALU.subtract).then_inc(signal, 1)

                dve.wait_ge(S["x_first"], 16 * (b + 1))
                first_statistics(0, 0)
                first_statistics(1, 1)
                first_norm(0, 0, 0)
                first_statistics(2, 0)
                values_out(0, 0, 0)
                norms(0, 0)
                first_norm(1, 1, 1)

                def tile(t, par, at):
                    n = b * NT + t
                    shifted(n, at, bank(0, 2), MXK, XSK, N2[:, par, NH:], S["xwk"], S["phik"], n, S["xk_sb"])
                    if at < NT - 2:
                        first_norm(t + 2, par, at + 2)
                    if at == 1:
                        dve.wait_ge(S["x_rest"], 16 * (NC - 1) * (b + 1))
                    if at < NT - 3:
                        first_statistics(t + 3, 1 - par)
                    if at < NT - 1:
                        values_out(t + 1, 1 - par, at + 1)
                        norms(t + 1, 1 - par)
                    shifted(n, at, bank(2, 2), MXQ, XSQ, N2[:, par, :NH], S["xwq"], S["eqt"], 2 * n, S["xq_sb"])

                over_tiles(dve, tile, own)
                dve.wait_ge(S["kv"], NT * (b + 1))
                v.tensor_copy(KVS[:].rearrange("p a j n -> p (a j n)"), bank(7)).then_inc(S["kv_sb"], 1)
                dve.wait_ge(S["kvT"], b + 1)
                kvt = bank(6).rearrange("p (a g n) -> p a g n", a=2, g=GR)
                for half, r in ((0, slice(0, NM)), (1, slice(NM, P))):
                    cols = slice(half * DK, (half + 1) * DK)
                    v.tensor_copy(NW[r, :, cols], kvt[r, 0, :, cols]).then_inc(S["kw_ok"], 1)
                    for j in range(2):
                        c = 2 * j + half
                        v.tensor_copy(DW[r, 4 * j:4 * j + 4, c:c + 1], kvt[r, 1, 4 * j:4 * j + 4, 0:1]
                                      ).then_inc(S["kw_ok"], 1)
                own(v.memset(MXN[:], 0.0))

                for it in range(NC + 3):
                    g = b * NC + it
                    if it < NC:
                        dve.wait_ge(S["denT"], g + 1)
                        own(v.tensor_scalar(R[:], bank(7).rearrange("p (i q n) -> p i q n", i=TPC, q=4)[:, :, :, 0:4],
                                            FAVOR_EPS, None, ALU.add))
                        own(v.reciprocal(R[:], R[:]))
                        for j in range(2):
                            rj = R[:].rearrange("p i q n -> p (i q) n")[:, :, 2 * j:2 * j + 2]
                            v.tensor_copy(RB[:, j].rearrange("p i (q h d) -> p (i q) h d", q=4, h=2),
                                          rj.rearrange("p a (h o) -> p a h o", o=1).broadcast_to([P, TPC * 4, 2, DK])
                                          ).then_inc(S["rb"], 1)
                    if 1 <= it <= NC:
                        dve.wait_ge(S["rstd2"], g)
                        for i in range(TPC):
                            t = (it - 1) * TPC + i
                            v_ins = centred(Hh[:, t], X[:, t], t)
                            if i < TPC - 1:
                                own(v_ins)
                        v_ins.then_inc(S["h2a"], 1)
                    if it < NC:
                        dve.wait_ge(S["rT"], g + 1)
                        if it > 0:
                            dve.wait_ge(S["yps"], g)
                        v.tensor_tensor(MT[:].rearrange("p j n -> p (j n)"), bank(4, 2),
                                        NUMS[:].rearrange("p j n -> p (j n)"), ALU.mult).then_inc(S["mt"], 1)
                    if it >= 3:
                        for n, t in blocks(it - 3):
                            dve.wait_ge(S["q_hi"], NQ * b + n + 1)
                            v.tensor_tensor(QKS[:, n % 3, 1], TMP[:, n % 2], QKS[:, n % 3, 0].bitcast(F32),
                                            ALU.subtract).then_inc(S["q_lo"], 1)
                    if 2 <= it < NC + 2:
                        dve.wait_ge(S["rstd3"], g - 1)
                        if it > 2:
                            dve.wait_ge(S["x2T"], g - 2)
                        for i in range(TPC):
                            t = (it - 2) * TPC + i
                            centred(X2[:, i], Hh[:, t], t).then_inc(S["x2"], 1)
                    if it >= 3:
                        for i in range(TPC):
                            n = NT * b + (it - 3) * TPC + i
                            dve.wait_ge(S["vp"], n + 1)
                            v.tensor_tensor(V2[:, expert[it - 3] * TPC + i], bank(i % 2)[:, 0:D], VB[:], ALU.add
                                            ).then_inc(S["v2_sb"], 1)
                    if it < NC:
                        dve.wait_ge(S["yps"], g + 1)
                        if it == 0:
                            dve.wait_ge(S["xb"], NT * (b + 1))
                        v.tensor_tensor(X[:, slot(it)], bank(6, 2).rearrange("p (t d) -> p t d", t=TPC), X[:, slot(it)],
                                        ALU.add).then_inc(S["x1"], 1)
                        dve.wait_ge(S["x1"], g + 1)
                        statistics(range(it * TPC, (it + 1) * TPC), [X[:, it * TPC + i] for i in range(TPC)], "ve2")
                    if 1 <= it <= NC:
                        dve.wait_ge(S["h2"], g)
                        statistics(range((it - 1) * TPC, it * TPC), [Hh[:, (it - 1) * TPC + i] for i in range(TPC)], "ve3")

                own(v.memset(NUM[2 * DH:, 2:4], 0.0))
                own(v.memset(NUM[DH:2 * DH, 3], 0.0))
                own(v.memset(SUM[2 * DH:, 2:4], 1.0))
                own(v.memset(SUM[DH:2 * DH, 3], 1.0))

                def maxima(p0, p1):
                    for p in range(p0, min(p1, NU * MAXU)):
                        u, m = divmod(p, MAXU)
                        dve.wait_ge(S["am"], NU * MAXU * b + p + 1)
                        v.tensor_reduce(MXP[:, u % 2, m // NC, m % NC:m % NC + 1], bank(m % 2), AX.X, ALU.max
                                        ).then_inc(S["am_rd"], 1)
                        if m == MAXU - 1:
                            dve.wait_ge(S["am_rd"], NU * MAXU * b + p + 1)
                            own(v.tensor_reduce(MXN[:, u % 2, 0:TPC], MXP[:, u % 2], AX.X, ALU.max, negate=True))
                            if u >= 2:
                                dve.wait_ge(shift[(u - 2) % 4], 64 * (SHN[(u - 2) % 4] * b + (u - 2) // 4 + 1))
                            v.transpose(MXT[:, u % 2], MXN[:, u % 2]).then_inc(S["mxt"], 1)

                def divide_part(z, q):
                    part = SUM[:, z, q * P:(q + 1) * P]
                    return v.reciprocal(part, part)

                def result(s):
                    e = expert[s]
                    m = width[e]
                    src = out_ps(e).rearrange("p (t d) -> p t d", t=TPC)
                    dve.wait_ge(S["ops"], b * NC + s + 1)
                    dve.wait_ge(S["base"], b * NC + s + 1)
                    v.tensor_tensor(X[:, slot(s), 0:m], src, X[:, slot(s), 0:m], ALU.add).then_inc(S["fin"], 1)

                maxima(0, LOOK)
                for u, (h, c) in enumerate(units):
                    for s in range(STEPS):
                        p = u * MAXU + s * 2 + LOOK
                        maxima(p, p + 2)
                        if s == 1 and u > 0:
                            finish(dve, v, b, u - 1)
                        for z, at in RECIPROCALS:
                            if u == at and s >= 4:
                                if s == 4:
                                    dve.wait_ge(S["c_out"], NU * b + u)
                                divide_part(z, s - 4).then_inc(S["rcp"], 1)
                        if u == NU - 1 and s in OUT_STEPS:
                            result(OUT_STEPS.index(s))
                finish(dve, v, b, NU - 1)
                dve.wait_ge(S["c_out"], NU * (b + 1))
                dve.wait_ge(S["fin_n"], NU * (b + 1))
                for q in range(TPC):
                    own(divide_part(NC, q))
                    part = slice(q * P, (q + 1) * P)
                    v.tensor_tensor(NUM[:, NC, part], NUM[:, NC, part], SUM[:, NC, part], ALU.mult
                                    ).then_inc(S["at_last"], 1)
                result(NC - 1)
                wait_apart(dve, (S["fin"], NC * (b + 1)))
                own.leave(B)

        @block.tensor
        def _(pe):
            mm, tr = nc.tensor.matmul, nc.tensor.transpose
            pe.wait_ge(S["id_ok"], 1)
            pe.wait_ge(S["w_in"], 16 * 8)
            for w in range(8):
                for k in range(KD):
                    for e in range(KD):
                        last = tr(bank(w)[:, k * D + e * P:k * D + (e + 1) * P], WN[:, w, e, k * P:(k + 1) * P], ident[:])
                last.then_inc(S["wT"], 1)
            pe.wait_ge(S["pj_in"], 16 * NH)
            for j in range(2):
                pe.wait_ge(S["wT_sb"], j + 1)
                for q in range(4):
                    last = tr(bank(j)[:, q * P:(q + 1) * P], PN[:, 4 * j + q], ident[:])
                last.then_inc(S["pT"], 1)
            pe.wait_ge(S["c_in"], 16 * (1 + KD))
            pe.wait_ge(S["sc_ok"], KD * B)
            pe.wait_ge(S["wT_sb"], 3)
            for m in range(2):
                for e in range(KD):
                    o = (m * KD + e) * B
                    for k in range(KD):
                        last = mm(bank(2)[:, o:o + B], WM[:, k, m * D + e * P:m * D + (e + 1) * P], SC[:, k],
                                  start=k == 0, stop=k == KD - 1)
            last.then_inc(S["mod"], 1)
            for b in range(B):
                pe.wait_ge(S["wT_sb"], 8)
                if b >= 2:
                    pe.wait_ge(S["mod_sb"], b - 1)
                for q in range(2):
                    for k in range(KD):
                        last = mm(bank(4 + b % 2 * 2 + q), SCB[:, k, b], WM[:, k, (q + 1) * CH:(q + 2) * CH],
                                  start=k == 0, stop=k == KD - 1)
                last.then_inc(S["mod"], 1)
            pe.wait_ge(S["setup_ok"], 1)

            with pe.Fori(0, B) as b:
                def x_transposes(t, par, at):
                    n = b * NT + t
                    pe.wait_ge(S["xh"], n + 1)
                    if at >= 1:
                        pe.wait_ge(S["v_sb"], n)
                    for k in range(KD):
                        last = tr(bank(6)[:, D + k * P:D + (k + 1) * P], XH[:, par, k * P:(k + 1) * P], ident[:])
                    last.then_inc(S["xT"], 1)

                def project(t, at):
                    n = b * NT + t
                    pe.wait_ge(S["hT"], KD * (n + 1))
                    if at >= 1:
                        pe.wait_ge(S["qkT_sb"], n)
                    for k in range(KD):
                        mm(bank(4), HT[:, k], W1T[:, k, 0:2 * D], start=k == 0, stop=k == KD - 1)
                    for k in range(KD):
                        last = mm(bank(6)[:, 0:D], HT[:, k], W1T[:, k, 2 * D:], start=k == 0, stop=k == KD - 1)
                    last.then_inc(S["qkv"], 1)

                def qk_transposes(t, at):
                    n = b * NT + t
                    pe.wait_ge(S["qk_sb"], n + 1)
                    pe.wait_ge(S["sq"], n + 1)
                    for q in range(4):
                        last = tr(bank(4)[:, q * P:(q + 1) * P], QK[:, q * P:(q + 1) * P], ident[:])
                    last.then_inc(S["qkT"], 1)

                def query_features(t, half, at):
                    n = b * NT + t
                    if half == 0:
                        pe.wait_ge(S["expq"], n + 1)
                        if at >= 1:
                            pe.wait_ge(S["phiq"], 2 * n)
                    else:
                        pe.wait_ge(S["phiq"], 2 * n + 1)
                    for q in range(4):
                        last = tr(bank(5)[:, q * P:(q + 1) * P], XSQ[:, (half * 4 + q) * P:(half * 4 + q + 1) * P], ident[:])
                    last.then_inc(S["eqt"], 1)

                def scores(n, at, base, o, ready, free):
                    if at >= 1:
                        pe.wait_ge(S[free], n)
                    for j in range(2):
                        last = mm(bank(base + j), QKT[:, o + j], PB[:, j], start=True, stop=True)
                    last.then_inc(S[ready], 1)

                def key_values(n, par, at):
                    pe.wait_ge(S["phik"], n + 1)
                    for a_ in range(2):
                        for j in range(2):
                            for q in range(4):
                                gr = 4 * j + q
                                W = V1[:, par, gr * 2 * DK:(gr + 1) * 2 * DK] if a_ == 0 else ones[:]
                                last = mm(bank(7)[32 * q:32 * q + 32, (2 * a_ + j) * P:(2 * a_ + j + 1) * P], W,
                                          PK[:, par, gr * P:(gr + 1) * P], start=at == 0 and a_ == 0 and j == 0,
                                          stop=at == NT - 1, skip_group_check=True, tile_position=(0, 32 * q))
                    last.then_inc(S["kv"], 1)

                x_transposes(0, 0, 0)
                project(0, 0)
                qk_transposes(0, 0)
                x_transposes(1, 1, 1)

                def tile(t, par, at):
                    n = b * NT + t
                    pe.wait_ge(S["qkT_sb"], n + 1)
                    scores(n, at, 0, 2, "xwk", "xk_sb")
                    if at < NT - 1:
                        project(t + 1, at + 1)
                    if at >= 1:
                        query_features(t - 1, 0, at - 1)
                    scores(n, at, 2, 0, "xwq", "xq_sb")
                    if at >= 1:
                        query_features(t - 1, 1, at - 1)
                    if at < NT - 1:
                        qk_transposes(t + 1, at + 1)
                    key_values(n, par, at)
                    if at < NT - 2:
                        x_transposes(t + 2, par, at + 2)

                over_tiles(pe, tile)
                query_features(NT - 1, 0, NT - 1)
                query_features(NT - 1, 1, NT - 1)
                pe.wait_ge(S["kv_sb"], b + 1)
                pe.wait_ge(S["v_sb"], NT * (b + 1))
                for a_ in range(2):
                    for j in range(2):
                        last = tr(bank(6)[:, (2 * a_ + j) * P:(2 * a_ + j + 1) * P], KVS[:, a_, j], ident[:])
                last.then_inc(S["kvT"], 1)
                pe.wait_ge(S["kw_ok"], 6 * (b + 1))
                pe.wait_ge(S["phiq"], 2 * NT * (b + 1))
                pe.wait_ge(S["xq_sb"], NT * (b + 1))

                for it in range(NC + 3):
                    g = b * NC + it
                    if it < NC:
                        if it > 0:
                            pe.wait_ge(S["x1"], g)
                        for j in range(2):
                            for q in range(4):
                                last = mm(bank(6)[32 * q:32 * q + 32, :], DW[:, 4 * j + q],
                                          PHIQ[:, 4 * j + q, it * CH:(it + 1) * CH], start=j == 0, stop=j == 1,
                                          tile_position=(0, 32 * q))
                        last.then_inc(S["den"], 1)
                        if it > 0:
                            pe.wait_ge(S["mt"], g)
                        for j in range(2):
                            for q in range(4):
                                last = mm(bank(4 + j)[32 * q:32 * q + 32, :], NW[:, 4 * j + q],
                                          PHIQ[:, 4 * j + q, it * CH:(it + 1) * CH], start=True, stop=True,
                                          tile_position=(0, 32 * q))
                        last.then_inc(S["num"], 1)
                        pe.wait_ge(S["den_sb"], g + 1)
                        for i in range(TPC):
                            last = tr(bank(7)[:, i * P:(i + 1) * P], DENS[:, i * P:(i + 1) * P], ident[:])
                        last.then_inc(S["denT"], 1)
                    if it >= 3:
                        s = it - 3
                        e = expert[s]
                        W = W2T if e < 2 else W2M
                        ks = [(k, k) for k in range(KD)] if e == 0 else [(0, 0 if e == 1 else e - 2)]
                        pe.wait_ge(S["xn_sb"], 2 * (b * NC + s + 1))
                        for n, t in blocks(s):
                            j, w = t % 2, (1 if t < 2 else 0)
                            if n >= 2:
                                pe.wait_ge(S["q_hi"], NQ * b + n - 1)
                            for q, (k, wk) in enumerate(ks):
                                last = mm(bank(2 + n % 2), W[:, wk, w * D + j * P:w * D + (j + 1) * P], XNT[:, k],
                                          start=q == 0, stop=q == len(ks) - 1)
                            last.then_inc(S["qp"], 1)
                    if it < NC:
                        pe.wait_ge(S["rb"], 2 * (g + 1))
                        pe.wait_ge(S["num_sb"], g + 1)
                        for j in range(2):
                            for i in range(TPC):
                                last = tr(bank(4 + j)[:, i * P:(i + 1) * P], RB[:, j, i], ident[:])
                        last.then_inc(S["rT"], 1)
                    if it >= 3:
                        for i in range(TPC):
                            n = NT * b + s * TPC + i
                            if i >= 2:
                                pe.wait_ge(S["v2_sb"], n - 1)
                            for q, (k, wk) in enumerate(ks):
                                last = mm(bank(i % 2)[:, 0:D], XNT[:, k, i * P:(i + 1) * P], W[:, wk, 2 * D:],
                                          start=q == 0, stop=q == len(ks) - 1)
                            last.then_inc(S["vp"], 1)
                    if it < NC:
                        pe.wait_ge(S["mt"], g + 1)
                        pe.wait_ge(S["gated"], 2 * (b + 1))
                        for i in range(TPC):
                            for j in range(2):
                                last = mm(bank(6, 2)[:, i * D:(i + 1) * D], MT[:, j, i * P:(i + 1) * P], WoG[:, j],
                                          start=j == 0, stop=j == 1)
                        last.then_inc(S["yps"], 1)
                    if 2 <= it < NC + 2:
                        pe.wait_ge(S["x2"], (g - 1) * TPC)
                        if it >= 3:
                            pe.wait_ge(S["v2_sb"], (g - 2) * TPC)
                        for i in range(TPC):
                            for k in range(KD):
                                last = tr(bank(k)[:, i * P:(i + 1) * P], X2[:, i, k * P:(k + 1) * P], ident[:])
                        last.then_inc(S["x2T"], 1)

                pe.wait_ge(S["q_hi"], NQ * (b + 1))
                pe.wait_ge(S["v2_sb"], NT * (b + 1))

                def maxima(p0, p1):
                    for p in range(p0, min(p1, NU * MAXU)):
                        u, m = divmod(p, MAXU)
                        h, c = units[u]
                        ks = heads.index(h) % 4
                        if m == 0:
                            pe.wait_ge(q_in[u % 4], 48 * (SHN[u % 4] * b + u // 4 + 1))
                            pe.wait_ge(k_in[ks], 48 * (2 * b + heads.index(h) // 4 + 1))
                        if p >= 2:
                            pe.wait_ge(S["am_rd"], NU * MAXU * b + p - 1)
                        mm(bank(m % 2), QOP[0:96, u % 4, m // NC * P:(m // NC + 1) * P],
                           KOP[0:96, ks, m % NC * CH:(m % NC + 1) * CH], start=True, stop=True).then_inc(S["am"], 1)

                def output(s):
                    e = expert[s]
                    m = width[e]
                    k = [z for z, _ in RECIPROCALS].index(e)
                    pe.wait_ge(S["at"], len(RECIPROCALS) * b + k + 1)
                    if e == 1:
                        pe.wait_ge(S["am_rd"], NU * MAXU * (b + 1))
                        pe.wait_ge(S["base"], NC * b + 1)
                    if e == 3:
                        pe.wait_ge(S["fin"], NC * b + 2)
                    for i in range(TPC):
                        o = out_ps(e)[:, i * m:(i + 1) * m]
                        last = mm(o, NUM[:, e, i * P:(i + 1) * P],
                                  OWG[:, 0, 0:m] if e == 1 else OWMG[:, e - 2, 0:m], start=True, stop=True)
                    last.then_inc(S["ops"], 1)

                maxima(0, LOOK)
                for u, (h, c) in enumerate(units):
                    n0 = (NU * b + u) * STEPS
                    ks = heads.index(h) % 4
                    pe.wait_ge(shift[u % 4], 64 * (SHN[u % 4] * b + u // 4 + 1))

                    def values(s):
                        pe.wait_ge(S["ex"], n0 + s + 1)
                        if s == 0 and u >= 2:
                            pe.wait_ge(S["c_out"], NU * b + u - 1)
                        for q in range(2):
                            kt = 2 * s + q
                            for z, W in ((0, V2[:, kt, h * DH:(h + 1) * DH]), (1, ones[:])):
                                r = 64 * q + 32 * z
                                last = mm(PS[r:r + DH, 6 + u % 2, :], W, PR[:, s % 2, q], start=s == 0,
                                          stop=s == STEPS - 1, tile_position=(0, r))
                        if s == STEPS - 1:
                            last.then_inc(S["cps"], 1)

                    for s in range(STEPS):
                        for q in range(2):
                            kt = 2 * s + q
                            last = mm(bank(2 + s % 2 * 2 + q), KOP[:, ks, kt * P:(kt + 1) * P], QOP[:, u % 4],
                                      start=True, stop=True)
                        last.then_inc(S["sc_b"], 1)
                        p = u * MAXU + s * 2 + LOOK
                        maxima(p, p + 2)
                        if s > 0:
                            values(s - 1)
                        if u == NU - 1 and s in OUT_STEPS:
                            output(OUT_STEPS.index(s))
                    values(STEPS - 1)
                pe.wait_ge(S["ex"], NU * STEPS * (b + 1))
                pe.wait_ge(S["at"], len(RECIPROCALS) * (b + 1))
                for i in range(TPC):
                    tok = slice(i * P, (i + 1) * P)
                    o = out_ps(0)[:, i * D:(i + 1) * D]
                    mm(o, NUM[:, 0, tok], OWG[:, 0], start=True, stop=False)
                    pe.wait_ge(S["at_last"], TPC * b + i + 1)
                    last = mm(o, NUM[:, NC, tok], OWG[:, 1], start=False, stop=True)
                last.then_inc(S["ops"], 1)


_INS = ['L0_attn_x', 'L0_attn_Wq', 'L0_attn_Wk', 'L0_attn_Wv', 'L0_attn_Wo', 'L0_attn_bo', 'L0_attn_proj',
        'L0_ffn_norm_w', 'L0_ffn_norm_b', 'L0_ffn_q_w', 'L0_ffn_q_b', 'L0_ffn_k_w', 'L0_ffn_k_b',
        'L0_ffn_v_w', 'L0_ffn_v_b', 'L0_ffn_o_w', 'L0_ffn_o_b', 'L0_c', 'L0_wmod']


def kernel(**inputs):
    import numpy as _np
    import concourse.bacc as _bacc
    from concourse import mybir as _mybir
    from concourse.bass_utils import run_bass_kernel_spmd as _run

    nc = _bacc.Bacc("TRN2", target_bir_lowering=False, num_devices=1)
    arrays, args = {}, []
    for name in _INS:
        a = _np.ascontiguousarray(inputs[name])
        arrays[f"in_{name}_dram"] = a
        args.append(nc.dram_tensor(f"in_{name}_dram", a.shape, _mybir.dt.from_np(a.dtype), kind="ExternalInput").ap())
    out = nc.dram_tensor("out_0_dram", inputs['L0_attn_x'].shape, F32, kind="ExternalOutput").ap()
    adaln_block(nc, *args, out)
    r = _run(nc, [arrays], core_ids=[0])
    return r.results[0]["out_0_dram"]
```

```python
from contextlib import ExitStack

import concourse.bass as bass
from concourse import mybir

F32 = mybir.dt.float32
F32R = mybir.dt.float32r
ALU = mybir.AluOpType
ACT = mybir.ActivationFunctionType
AX = mybir.AxisListType

P = 128
CH = 512
TPC = CH // P

PARTS = ((0, 0), (0, 1), (1, 0))

FAVOR_EPS = 1e-6
NORM_EPS = 1e-5
FLOOR = 0.25


class Chain:

    def __init__(self, eng, sem, passed=None):
        self.passed = passed
        self.eng, self.sem, self.base, self.n, self.outer = eng, sem, 0, 0, []

    def __call__(self, ins):
        ins.then_inc(self.sem, 1)
        self.n += 1
        self.eng.wait_ge(self.sem, self.base + self.n)
        if self.passed is not None:
            self.eng.sem_inc(self.passed, 1)

    def enter(self, i, per):
        self.outer.append((self.base, self.n, per))
        self.base, self.n = self.base + self.n + i * per, 0

    def leave(self, trips):
        assert self.n == self.outer[-1][2], self.n
        self.base, n, per = self.outer.pop()
        self.n = n + per * trips


def adaln_block(nc, x, Wq, Wk, Wv, Wo, bo, proj, norm_w, norm_b, q_w, q_b, k_w, k_b, v_w, v_b, o_w, o_b,
                cond, wmod, out):
    B, T, D = x.shape
    NH, NM, DK = proj.shape
    H2N, EXPERTS = 8, 4
    DH = D // H2N
    KD = D // P
    NT, NC = T // P, T // CH
    GR = NH * NM // P
    assert NC == EXPERTS and NT == NC * TPC and KD == 2 and GR == 8
    PHI = 1.0 / NM ** 0.5
    QS = 1.0 / DK ** 0.5
    SCALE = float(D) ** -0.5
    width = [D >> e for e in range(EXPERTS)]

    expert = (1, 2, 0, 3)
    slot_of = {e: s for s, e in enumerate(expert)}
    results = (1, 2, 3, 0)
    units = [(h, c) for h in range(H2N) for c in (expert if h == 0 else range(NC)) if h * DH < width[c]]
    NU = len(units)
    KT = T // P
    STEPS = KT // 2
    MAXU = TPC * NC
    loads_of = {}
    for u, (h, c) in enumerate(units):
        loads_of.setdefault(h, u)

    NQ = 3 * NC + 1
    QSN = [len(range(i, NQ, 3)) for i in range(3)]
    SHN = [len(range(i, NU, 4)) for i in range(4)]
    LOOK, EARLY = 24, 3
    firsts = [(u, expert[s]) for u, s in ((0, 0), (0, 1), (0, 2), (1, 0), (0, 3), (1, 1), (1, 2), (1, 3))]
    stream = [(u, i, kc) for u, kc in firsts for i in range(TPC)]
    stream += [(u, i, kc) for u in range(2, NU) for i in range(TPC) for kc in range(NC)]
    last_of = {u: p for p, (u, _, _) in enumerate(stream)}
    RECIPROCALS = ((3, 5), (2, 8), (0, 11), (1, 12))
    OUT_STEPS = (2, 4, 6)
    PER_B, PER_C, PER_P = 206, 12, 9


    k_scr = nc.dram_tensor("k_scr", (2, D, T), F32, kind="Internal").ap()
    q_scr = nc.dram_tensor("q_scr", (2, D, T), F32, kind="Internal").ap()

    with ExitStack() as ctx:
        def sb(name, shape, dt=F32, stack=ctx):
            return stack.enter_context(nc.sbuf_tensor(name, shape, dt))

        def sem(name):
            return ctx.enter_context(nc.semaphore(name))

        X = sb("X", [P, NT, D])
        W1T = sb("W1T", [P, 2, KD, 2 * D], F32R)
        WvT = sb("WvT", [P, KD, D])
        WoT = sb("WoT", [P, KD, D])
        WoG, BOG = sb("WoG", [P, KD, D]), sb("BOG", [P, D])
        W2T = sb("W2T", [P, KD, 3 * D])
        OWT = sb("OWT", [P, KD, D])
        OWG = sb("OWG", [P, KD, D])
        PB = sb("PB", [P, 2, 2, CH], F32R)
        MODB = sb("MODB", [P, B, 4, D])
        MODC = sb("MODC", [P, 2, KD, B])
        BO, VB, OB = sb("BO", [P, D]), sb("VB", [P, D]), sb("OB", [P, D])
        COLS = sb("COLS", [P, 4, KD])
        COLM = sb("COLM", [P, 2, 2])
        QBS = sb("QBS", [P, KD])
        ident = sb("ident", [P, P])
        ones = sb("ones", [P, DH])
        minus_half = sb("minus_half", [P, NT])
        STAT = sb("STAT", [P, NT, 6])
        MV = sb("MV", [P, NT, 2])
        VE = sb("VE", [P, NT])
        RSTD = sb("RSTD", [P, NT])
        NW, DW = sb("NW", [P, GR, 32]), sb("DW", [P, GR, 32])

        s0 = ExitStack()
        WN = sb("WN", [P, 8, KD, D], stack=s0)
        PN = sb("PN", [P, GR, P], stack=s0)
        WM = sb("WM", [P, KD, 6 * D], stack=s0)
        CT = sb("CT", [P, KD, B], stack=s0)
        CE = sb("CE", [P, KD, B], stack=s0)
        SC = sb("SC", [P, KD, B], stack=s0)
        SCB = sb("SCB", [P, KD, B, P], stack=s0)
        GS = sb("GS", [P, 2, 2, D], stack=s0)
        s0.close()

        s1 = ExitStack()
        QOP = sb("QOP", [97, 4, CH], F32R, stack=s1)
        KOP = sb("KOP", [97, 4, T], F32R, stack=s1)
        PR = sb("PR", [P, 2, 2, CH], stack=s1)
        CS = sb("CS", [2 * DH, 2, CH], stack=s1)
        SUM = sb("SUM", [P, NC + 1, CH], stack=s1)
        s1.close()
        PHIQ = sb("PHIQ", [P, GR, T])

        s2 = ExitStack()
        XH = sb("XH", [P, 2, D], stack=s2)
        HT = sb("HT", [P, KD, P], stack=s2)
        HTR = sb("HTR", [P, 2, KD, P], F32R, stack=s2)
        QK = sb("QK", [P, 2 * D], stack=s2)
        SQ = sb("SQ", [P, 2 * D], stack=s2)
        N2 = sb("N2", [P, 2, 2 * NH], stack=s2)
        QKT = sb("QKT", [P, 2, 4, P], F32R, stack=s2)
        MXK, MXQ = sb("MXK", [P, NH], stack=s2), sb("MXQ", [P, NH], stack=s2)
        XSK = sb("XSK", [P, NH * NM], stack=s2)
        XSQ = sb("XSQ", [P, NH * NM], stack=s2)
        PK = sb("PK", [P, 2, NH * NM], stack=s2)
        V1 = sb("V1", [P, 2, D], stack=s2)
        STAT1, MV1 = sb("STAT1", [P, 2, 6], stack=s2), sb("MV1", [P, 2, 2], stack=s2)
        VE1, RSTD1 = sb("VE1", [P, 2], stack=s2), sb("RSTD1", [P, 2], stack=s2)
        s2.close()

        V2 = sb("V2", [P, KT, D])
        Hh = sb("Hh", [P, NT, D])
        X2 = sb("X2", [P, TPC, D])
        XNT = sb("XNT", [P, KD, CH])
        TMP = sb("TMP", [P, 2, CH])
        QKS = sb("QKS", [P, 3, 2, CH], F32R)
        MXP = sb("MXP", [P, 2, TPC, NC])
        MXN = sb("MXN", [P, 2, 32])
        MXT = sb("MXT", [P, 2, 32])
        s3 = ExitStack()
        NUM = sb("NUM", [P, NC + 1, CH], stack=s3)
        s3.close()
        DENS = sb("DENS", [P, CH])
        KVS = DENS[:].rearrange("p (a j n) -> p a j n", a=2, j=2)
        NUMS = sb("NUMS", [P, 2, CH])
        R = sb("R", [P, TPC, 2, 4, 2])
        RB = sb("RB", [P, TPC, 2, P])
        MT = sb("MT", [P, 2, CH])

        PS = ctx.enter_context(nc.psum_tensor("PS", [P, 8, CH], F32))

        def bank(i, n=1):
            return PS[:, i:i + n, :].rearrange("p b n -> p (b n)")

        def out_ps(e):
            if e == 0:
                return bank(4, 2)
            return bank(0) if e == 1 else bank(1)[:, (0 if e == 2 else 4 * width[2]):][:, 0:TPC * width[e]]

        names = """w_in c_in vec_in pj_in id0 id_ok nb0 mh_ok mk0
                   wT wT_sb pT sig sc_ok mod mod_sb setup_ok
                   x_first x_rest ve1 rstd1 xh xT hT hT_hi hT_lo qkv qk_sb sq v_sb n2 qkT qkT_sb qkT_lo xwk xwq xk_sb xq_sb expk expq
                   phik kv kv_sb eqt kvT phiq gated xb kw_ok
                   den den_sb num num_sb denT rec rb rT mt yps x1
                   ve2 rstd2 ve3 rstd3 h2a h2m h2 x2 x2T xn_sb qp q_tmp q_hi q_lo scr0 scr1 scr2 vp v2_sb init_ok
                   q_in0 q_in1 q_in2 q_in3 kf0 kf1 kf2 kf3 k_in0 k_in1 k_in2 k_in3 am am_rd mxt shift0 shift1 shift2 shift3
                   sc_b ex cps cs_up c_out pool_own rcp at at_last base ops fin st0 st1 st2 st3 fin_n dve_own passed""".split()
        S = {n: sem(n) for n in names}
        q_in = [S[f"q_in{i}"] for i in range(4)]
        k_in = [S[f"k_in{i}"] for i in range(4)]
        shift = [S[f"shift{i}"] for i in range(4)]

        block = ctx.enter_context(nc.Block())
        xv = x.rearrange("b (c t p) d -> p (b c) t d", p=P, t=TPC)
        ov = out.rearrange("b (c t p) d -> p (b c) t d", p=P, t=TPC)
        heads = sorted(loads_of)
        last_unit = {h: max(u for u, (hh, _) in enumerate(units) if hh == h) for h in heads}
        scr = [S[f"scr{i}"] for i in range(3)]
        st = [S[f"st{i}"] for i in range(NC)]

        def slot(s):
            return slice(s * TPC, (s + 1) * TPC)

        def blocks(s):
            n0 = 3 * s + (1 if s > slot_of[0] else 0)
            return [(n0 + t, t) for t in ((0, 1, 2, 3) if expert[s] == 0 else (0, 1, 2))]

        def max_bank(p):
            return p % 2 if p >= LOOK else 4 + p % 4

        def keys_there(b, h):
            i = heads.index(h)
            return k_in[i % 4], 48 * (b + 1 if i % 4 == 0 else 2 * b + i // 4 + 1)

        def stored(b, n):
            return scr[n % 3], 32 * (QSN[n % 3] * b + n // 3 + 1)

        def over_tiles(eng, tile, own=None):
            for t in range(2):
                tile(t, t, t)
            with eng.Fori(0, NT // 2 - 3) as i:
                if own is not None:
                    own.enter(i, PER_C)
                for par in range(2):
                    tile(i * 2 + 2 + par, par, NT // 2)
                if own is not None:
                    own.leave(NT // 2 - 3)
            for t in range(NT - 4, NT):
                tile(t, t % 2, t)

        def wait_apart(eng, *waits):
            for s_, value in waits:
                eng.wait_ge(s_, value)
                eng.sem_inc(S["passed"], 1)

        @block.sync
        def _(sp):
            for w, src in enumerate((Wq, Wk, Wv, Wo, q_w, k_w, v_w, o_w)):
                sp.dma_start(WN[:, w], src.rearrange("(e p) d -> p e d", p=P)).then_inc(S["w_in"], 16)
            sp.dma_start(WM[:], wmod.rearrange("(k p) n -> p k n", p=P)).then_inc(S["c_in"], 16)
            for k in range(KD):
                sp.dma_start(CT[:, k], cond[:, k * P:(k + 1) * P].rearrange("b p -> p b"),
                             allow_slow_non_contiguous=True).then_inc(S["c_in"], 16)
            for dst, src in ((BO, bo), (VB, v_b), (OB, o_b)):
                sp.dma_start(dst[:], src.rearrange("(a n) -> a n", a=1).broadcast_to([P, D])).then_inc(S["vec_in"], 16)
            for n, src in enumerate((norm_w, norm_b, q_b, k_b)):
                sp.dma_start(COLS[:, n], src.rearrange("(k p) -> p k", p=P),
                             allow_slow_non_contiguous=True).then_inc(S["vec_in"], 16)
            sp.wait_ge(S["nb0"], 1)
            for h in range(NH):
                r, c = h % 2 * NM, h % 8 * DK
                sp.dma_start(PN[r:r + NM, h // 2, c:c + DK], proj[h]).then_inc(S["pj_in"], 16)

            def load_x(b, s):
                sp.dma_start(X[:, slot(s)], xv[:, bass.ds(b * NC + expert[s], 1)].rearrange("p o t d -> p (o t) d")
                             ).then_inc(S["x_first" if s == 0 else "x_rest"], 16)

            for s in range(NC):
                load_x(0, s)

            def load_q(b, u):
                h, c = units[u]
                for r, half in ((0, 0), (32, 1), (64, 0)):
                    sp.dma_start(QOP[r:r + DH, u % 4].bitcast(F32),
                                 q_scr[half, h * DH:(h + 1) * DH, c * CH:(c + 1) * CH]).then_inc(q_in[u % 4], 16)

            def batch(b, last):
                for s in range(NC):
                    e = expert[s]
                    for n, t in blocks(s):
                        dst, j = (k_scr, t) if t < 2 else (q_scr, t - 2)
                        sp.wait_ge(S["q_lo"], NQ * b + n + 1)
                        for half in range(2):
                            sp.dma_start(dst[half, j * P:(j + 1) * P, e * CH:(e + 1) * CH],
                                         QKS[:, n % 3, half].bitcast(F32)).then_inc(scr[n % 3], 16)
                    n0 = blocks(s)[0][0]
                    wait_apart(sp, stored(b, n0), stored(b, n0 + 2))
                    for r, half in ((0, 0), (32, 0), (64, 1)):
                        sp.dma_start(KOP[r:r + DH, 0, e * CH:(e + 1) * CH].bitcast(F32),
                                     k_scr[half, 0:DH, e * CH:(e + 1) * CH]).then_inc(S[f"kf{e}"], 16)
                    load_q(b, s)

                def load_k(h):
                    s = heads.index(h) % 4
                    for r, half in ((0, 0), (32, 0), (64, 1)):
                        sp.dma_start(KOP[r:r + DH, s].bitcast(F32),
                                     k_scr[half, h * DH:(h + 1) * DH, :]).then_inc(k_in[s], 16)

                def load_shift(u):
                    sp.wait_ge(S["mxt"], NU * b + u + 1)
                    for g in range(4):
                        dst = QOP[96:97, u % 4, :].bitcast(F32).rearrange("o (t g n) -> o t g n", t=TPC, g=4)[:, :, g]
                        sp.dma_start(dst, MXT[32 * g:32 * g + TPC, u % 2, :]).then_inc(shift[u % 4], 16)

                wait_apart(sp, *[stored(b, n) for n in range(NQ - 3, NQ)], (S["init_ok"], b + 1))
                for h in heads[1:4]:
                    load_k(h)
                loaded_k = set(heads[0:4])
                load_shift(0)
                for u in range(NU):
                    if u + 1 < NU:
                        load_shift(u + 1)
                    if u < NU - 1:
                        wait_apart(sp, (S["sc_b"], STEPS * (NU * b + u + 1)))
                    if u + 4 < NU:
                        load_q(b, u + 4)
                    for h in heads[4:]:
                        if h not in loaded_k and last_unit[heads[heads.index(h) - 4]] <= u:
                            load_k(h)
                            loaded_k.add(h)
                for k, e in enumerate(results):
                    s = slot_of[e]
                    sp.wait_ge(S["fin"], NC * b + k + 1)
                    sp.dma_start(ov[:, bass.ds(b * NC + e, 1)].rearrange("p o t d -> p (o t) d"),
                                 X[:, slot(s)]).then_inc(st[s], 16)
                    if k > 0 and not last:
                        wait_apart(sp, (st[slot_of[results[k - 1]]], 16 * (b + 1)))
                        load_x(b + 1, slot_of[results[k - 1]])
                if not last:
                    wait_apart(sp, (st[slot_of[results[-1]]], 16 * (b + 1)))
                    load_x(b + 1, slot_of[results[-1]])

            with sp.Fori(0, B - 1) as b:
                batch(b, False)
            batch(B - 1, True)
            for s in range(NC):
                sp.wait_ge(st[s], 16 * B)

        @block.gpsimd
        def _(pool):
            g = nc.gpsimd
            g.memset(PN[:], 0.0).then_inc(S["nb0"], 1)
            g.memset(ident[:], 0.0).then_inc(S["id0"], 1)
            pool.wait_ge(S["id0"], 1)
            g.affine_select(out=ident[:], in_=ident[:], compare_op=ALU.not_equal, fill=1.0, base=0,
                            pattern=[[-1, P]], channel_multiplier=1).then_inc(S["id_ok"], 1)
            g.memset(minus_half[:], -0.5).then_inc(S["mh_ok"], 1)
            g.memset(ones[:], 1.0).then_inc(S["mh_ok"], 1)
            g.memset(COLM[:], 0.0).then_inc(S["mk0"], 1)
            pool.wait_ge(S["mh_ok"], 2)
            pool.wait_ge(S["setup_ok"], 1)
            with pool.Fori(0, B) as b:
                def rsqrt(cols, ready, signal, n):
                    wait_apart(pool, (S[ready], n))
                    g.tensor_tensor(RSTD[:, cols], VE[:, cols], minus_half[:, cols], ALU.pow).then_inc(S[signal], 1)

                def rsqrt_tile(t, par):
                    wait_apart(pool, (S["ve1"], b * NT + t + 1))
                    g.tensor_tensor(RSTD1[:, par:par + 1], VE1[:, par:par + 1], minus_half[:, 0:1], ALU.pow
                                    ).then_inc(S["rstd1"], 1)

                rsqrt_tile(0, 0)
                gate = MODB[:, bass.ds(b, 1), 0, :]
                g.tensor_tensor(WoG[:], WoT[:], gate.broadcast_to([P, KD, D]), ALU.mult).then_inc(S["gated"], 1)
                g.tensor_tensor(BOG[:], BO[:], gate.rearrange("p o d -> p (o d)"), ALU.mult).then_inc(S["gated"], 1)

                rsqrt_tile(1, 1)
                rsqrt_tile(2, 0)

                def low_h(t):
                    n = b * NT + t
                    wait_apart(pool, (S["hT"], KD * (n + 1)), (S["hT_hi"], KD * (n + 1)))
                    g.tensor_tensor(HTR[:, 1], HT[:], HTR[:, 0].bitcast(F32), ALU.subtract).then_inc(S["hT_lo"], 1)

                low_h(0)
                low_h(1)

                def tile(t, par, at):
                    n = b * NT + t
                    if at >= 2:
                        wait_apart(pool, (S["kv"], n - 1))
                    wait_apart(pool, (S["expk"], n + 1))
                    g.tensor_scalar(PK[:, par], XSK[:], FAVOR_EPS, PHI, ALU.add, ALU.mult).then_inc(S["phik"], 1)
                    if at < NT - 3:
                        rsqrt_tile(t + 3, 1 - par)
                    wait_apart(pool, (S["xh"], n + 1), (S["gated"], 2 * (b + 1)))
                    src = X[:, bass.ds(t, 1)].rearrange("p t d -> p (t d)")
                    g.tensor_tensor(src, src, BOG[:], ALU.add).then_inc(S["xb"], 1)
                    if at < NT - 2:
                        low_h(t + 2)

                over_tiles(pool, tile)
                for it in range(NC + 1):
                    if 1 <= it < NC:
                        s = it - 1
                        for op, m, ready, signal in ((ALU.mult, 2, "h2a", "h2m"), (ALU.add, 1, "h2m", "h2")):
                            wait_apart(pool, (S[ready], (NC if ready == "h2a" else NC - 1) * b + s + 1))
                            g.tensor_tensor(Hh[:, slot(s)], Hh[:, slot(s)],
                                            MODB[:, bass.ds(b, 1), m, :].broadcast_to([P, TPC, D]), op
                                            ).then_inc(S[signal], 1)
                    if it < NC:
                        rsqrt(slot(it), "ve2", "rstd2", NC * b + it + 1)
                    if it >= 1:
                        rsqrt(slot(it - 1), "ve3", "rstd3", NC * b + it)
                wait_apart(pool, (S["num"], 2 * NC * (b + 1)), (S["rstd3"], NC * (b + 1)))
                g.memset(KOP[96:97].bitcast(F32), 1.0).then_inc(S["init_ok"], 1)

                wait_apart(pool, (S["x2"], NT * (b + 1)), (S["init_ok"], b + 1))
                own_g = Chain(pool, S["pool_own"], S["passed"])
                own_g.enter(b, PER_P)
                gate = MODB[:, bass.ds(b, 1), 3, :]
                own_g(g.tensor_tensor(OWG[:], OWT[:], gate.broadcast_to([P, KD, D]), ALU.mult))
                for e in results:
                    s, m = slot_of[e], width[e]
                    own_g(g.tensor_tensor(Hh[:, slot(s), 0:m], Hh[:, slot(s), 0:m], OB[:, 0:m]
                                          .rearrange("p (o d) -> p o d", o=1).broadcast_to([P, TPC, m]), ALU.add))
                    own_g(g.tensor_tensor(Hh[:, slot(s)], Hh[:, slot(s)], gate.broadcast_to([P, TPC, D]), ALU.mult))
                    g.tensor_tensor(X[:, slot(s)], X[:, slot(s)], Hh[:, slot(s)], ALU.add).then_inc(S["base"], 1)
                own_g.leave(B)
                for k, (z, _) in enumerate(RECIPROCALS):
                    wait_apart(pool, (S["rcp"], TPC * (len(RECIPROCALS) * b + k + 1)))
                    g.tensor_tensor(NUM[:, z], NUM[:, z], SUM[:, z], ALU.mult).then_inc(S["at"], 1)
        @block.scalar
        def _(act):
            a = nc.scalar
            act.wait_ge(S["c_in"], 16 * (1 + KD))
            a.activation(CE[:], CT[:], ACT.Exp, scale=-1.0).then_inc(S["sig"], 1)
            act.wait_ge(S["setup_ok"], 1)
            with act.Fori(0, B) as b:
                def modulated(t, at):
                    n = b * NT + t
                    waits = [(S["xT"], n + 1)]
                    if at >= 1:
                        waits.append((S["qkv"], n))
                    wait_apart(act, *waits)
                    for k in range(KD):
                        a.activation(HT[:, k], bank(6)[:, D + k * P:D + (k + 1) * P], ACT.Identity,
                                     bias=MODC[:, 0, k, bass.ds(b, 1)], scale=MODC[:, 1, k, bass.ds(b, 1)]
                                     ).then_inc(S["hT"], 1)
                        a.activation(HTR[:, 0, k], bank(6)[:, D + k * P:D + (k + 1) * P], ACT.Identity,
                                     bias=MODC[:, 0, k, bass.ds(b, 1)], scale=MODC[:, 1, k, bass.ds(b, 1)]
                                     ).then_inc(S["hT_hi"], 1)

                def project(t, at):
                    n = b * NT + t
                    act.wait_ge(S["qkv"], n + 1)
                    if at >= 1:
                        act.wait_ge(S["qkT"], n)
                    a.activation(QK[:], bank(4), ACT.Copy).then_inc(S["qk_sb"], 1)

                def squares(t, at):
                    n = b * NT + t
                    if at >= 1:
                        act.wait_ge(S["n2"], n)
                    a.activation(SQ[:], bank(4), ACT.Square).then_inc(S["sq"], 1)

                def transposed(t, at):
                    n = b * NT + t
                    act.wait_ge(S["qkT"], n + 1)
                    if at >= 1:
                        act.wait_ge(S["xwq"], n)
                    a.activation(QKT[:, 0].rearrange("p a n -> p (a n)"), bank(4), ACT.Copy).then_inc(S["qkT_sb"], 1)

                def values_out(t, par, at):
                    n = b * NT + t
                    if at >= 2:
                        act.wait_ge(S["kv"], n - 1)
                    a.activation(V1[:, par], bank(6)[:, 0:D], ACT.Copy).then_inc(S["v_sb"], 1)

                def query_features(t, half):
                    wait_apart(act, (S["eqt"], 2 * (b * NT + t) + half + 1))
                    a.activation(PHIQ[:, half * 4:half * 4 + 4, bass.ds(t * P, P)],
                                 bank(5).rearrange("p (g n) -> p g n", g=4), ACT.Copy, bias=FAVOR_EPS * PHI,
                                 scale=PHI).then_inc(S["phiq"], 1)

                modulated(0, 0)
                project(0, 0)
                squares(0, 0)
                transposed(0, 0)
                values_out(0, 0, 0)
                modulated(1, 1)

                def tile(t, par, at):
                    n = b * NT + t
                    if at >= 1:
                        query_features(t - 1, 0)
                    act.wait_ge(S["xk_sb"], n + 1)
                    a.activation(XSK[:], XSK[:], ACT.Exp).then_inc(S["expk"], 1)
                    if at < NT - 1:
                        project(t + 1, at + 1)
                    if at < NT - 1:
                        squares(t + 1, at + 1)
                    if at < NT - 1:
                        values_out(t + 1, 1 - par, at + 1)
                    if at >= 1:
                        query_features(t - 1, 1)
                    if at < NT - 1:
                        transposed(t + 1, at + 1)
                    if at < NT - 2:
                        modulated(t + 2, at + 2)
                    act.wait_ge(S["xq_sb"], n + 1)
                    a.activation(XSQ[:], XSQ[:], ACT.Exp).then_inc(S["expq"], 1)

                over_tiles(act, tile)
                query_features(NT - 1, 0)
                query_features(NT - 1, 1)

                for it in range(NC + 3):
                    if it < NC:
                        g = b * NC + it
                        act.wait_ge(S["den"], g + 1)
                        if it > 0:
                            act.wait_ge(S["denT"], g)
                        a.activation(DENS[:], bank(6), ACT.Copy).then_inc(S["den_sb"], 1)
                        for j in range(2):
                            act.wait_ge(S["num"], 2 * g + j + 1)
                            if it > 0 and j == 0:
                                act.wait_ge(S["mt"], 2 * g)
                            a.activation(NUMS[:, j], bank(4 + j), ACT.Copy).then_inc(S["num_sb"], 1)
                        act.wait_ge(S["rec"], g + 1)
                        if it > 0:
                            act.wait_ge(S["rT"], 2 * g)
                        for i2 in range(2):
                            half = slice(2 * i2, 2 * i2 + 2)
                            src = R[:, half].rearrange("p i j q (h o) -> p (i j q h) o", o=1)
                            a.activation(RB[:, half].rearrange("p i j (g d) -> p (i j g) d", d=DK),
                                         src.broadcast_to([P, 4 * 2 * 4, DK]), ACT.Copy).then_inc(S["rb"], 1)
                    if it >= 3:
                        for n, t in blocks(it - 3):
                            j = t % 2
                            act.wait_ge(S["qp"], NQ * b + n + 1)
                            if n >= 2:
                                act.wait_ge(S["q_lo"], NQ * b + n - 1)
                            if n >= 3:
                                act.wait_ge(*stored(b, n - 3))
                            if t >= 2:
                                kw = dict(bias=QBS[:, j:j + 1], scale=SCALE)
                            else:
                                kw = dict(bias=COLS[:, 3, j:j + 1])
                            a.activation(TMP[:, n % 2], bank(2 + n % 2), ACT.Identity, **kw).then_inc(S["q_tmp"], 1)
                            a.activation(QKS[:, n % 3, 0], bank(2 + n % 2), ACT.Identity, **kw).then_inc(S["q_hi"], 1)
                    if 2 <= it < NC + 2:
                        act.wait_ge(S["x2T"], b * NC + it - 1)
                        e = expert[it - 2]
                        for k in range(KD if e == 0 else 1):
                            weight, bias = ((COLM[:, e - 2, 0:1], COLM[:, e - 2, 1:2]) if e >= 2 else
                                            (COLS[:, 0, k:k + 1], COLS[:, 1, k:k + 1]))
                            a.activation(XNT[:, k], bank(k), ACT.Identity, bias=bias, scale=weight
                                         ).then_inc(S["xn_sb"], 1)
                def odd_sum(u):
                    act.wait_ge(S["cps"], NU * b + u + 1)
                    if u >= 2:
                        act.wait_ge(S["c_out"], NU * b + u - 1)
                    a.activation(CS[:, u % 2], PS[2 * DH:4 * DH, 6 + u % 2, :], ACT.Copy).then_inc(S["cs_up"], 1)

                for u in range(NU):
                    n0 = (NU * b + u) * STEPS
                    for s in range(STEPS):
                        act.wait_ge(S["sc_b"], n0 + s + 1)
                        a.activation(PR[:, s % 2].rearrange("p a n -> p (a n)"), bank(2 + s % 2 * 2, 2),
                                     ACT.Exp).then_inc(S["ex"], 1)
                        if s == 1 and u > 0:
                            odd_sum(u - 1)
                odd_sum(NU - 1)

        def finish(dve, v, b, u):
            h, c = units[u]
            z = NC if h >= 4 else c
            r = h % 4 * DH
            dve.wait_ge(S["cs_up"], NU * b + u + 1)
            v.tensor_tensor(NUM[r:r + DH, z], PS[0:DH, 6 + u % 2, :], CS[0:DH, u % 2], ALU.add).then_inc(S["fin_n"], 1)
            v.tensor_tensor(SUM[r:r + DH, z], PS[DH:2 * DH, 6 + u % 2, :], CS[DH:2 * DH, u % 2], ALU.add
                            ).then_inc(S["c_out"], 1)

        @block.vector
        def _(dve):
            v = nc.vector
            own = Chain(dve, S["dve_own"])
            dve.wait_ge(S["sig"], 1)
            own(v.tensor_scalar_add(CE[:], CE[:], 1.0))
            own(v.reciprocal(SC[:], CE[:]))
            own(v.tensor_tensor(SC[:], SC[:], CT[:], ALU.mult))
            for k in range(KD):
                for b in range(B):
                    v.tensor_copy(SCB[:, k, b], SC[:, k, b:b + 1].broadcast_to([P, P])).then_inc(S["sc_ok"], 1)
            dests = [(W1T, 0, QS), (W1T, 1, QS), (WvT, 0, 1.0), (WoT, 0, 1.0),
                     (W2T, 0, 1.0), (W2T, 1, 1.0), (W2T, 2, 1.0), (OWT, 0, 1.0)]
            for w, (dst, o, s) in enumerate(dests):
                dve.wait_ge(S["wT"], w + 1)
                if w < 2:
                    cols, src = slice(o * D, (o + 1) * D), bank(w).rearrange("p (k n) -> p k n", k=KD)
                    own(v.tensor_scalar(dst[:, 0, :, cols], src, s, None, ALU.mult))
                    v.scalar_tensor_tensor(dst[:, 1, :, cols], src, s, dst[:, 0, :, cols].bitcast(F32), ALU.mult,
                                           ALU.subtract).then_inc(S["wT_sb"], 1)
                    continue
                v.tensor_scalar(dst[:, :, o * D:(o + 1) * D], bank(w).rearrange("p (k n) -> p k n", k=KD), s, None,
                                ALU.mult).then_inc(S["wT_sb"], 1)
            for j in range(2):
                dve.wait_ge(S["pT"], j + 1)
                own(v.tensor_copy(PB[:, 0, j], bank(j)))
                own(v.tensor_tensor(PB[:, 1, j], bank(j), PB[:, 0, j].bitcast(F32), ALU.subtract))
            dve.wait_ge(S["wT_sb"], 8)
            dve.wait_ge(S["vec_in"], 16 * 7)
            dve.wait_ge(S["mk0"], 1)
            for e in (2, 3):
                own(v.tensor_copy(COLM[0:width[e], e - 2], COLS[0:width[e], 0:2, 0]))
            own(v.tensor_scalar(QBS[:], COLS[:, 2], SCALE, None, ALU.mult))
            dve.wait_ge(S["mod"], 1)
            fm = bank(2)[:, 0:2 * KD * B].rearrange("p (m k b) -> p m k b", m=2, k=KD)
            own(v.tensor_copy(MODC[:, 0], fm[:, 0]))
            own(v.tensor_scalar(MODC[:, 1], fm[:, 1], 1.0, None, ALU.add))
            for b in range(B):
                dve.wait_ge(S["mod"], b + 2)
                own(v.tensor_copy(MODB[:, b].rearrange("p m d -> p (m d)"), bank(4 + b % 2 * 2, 2)))
                v.tensor_scalar(MODB[:, b, 2], MODB[:, b, 2], 1.0, None, ALU.add).then_inc(S["mod_sb"], 1)
                gate, t0, t1 = MODB[:, b, 0:4:3], GS[:, 0], GS[:, 1]
                own(v.tensor_scalar(t0, gate, 0.0, 2.0, ALU.is_ge, ALU.mult))
                own(v.tensor_scalar(t0, t0, -1.0, None, ALU.add))
                own(v.scalar_tensor_tensor(t1, gate, -1.0, gate, ALU.mult, ALU.max))
                own(v.scalar_tensor_tensor(gate, t1, FLOOR, t0, ALU.max, ALU.mult))
            dve.wait_ge(S["mod_sb"], B)
            v.tensor_copy(VE[:, 0:1], QBS[:, 0:1]).then_inc(S["setup_ok"], 1)
            dve.wait_ge(S["setup_ok"], 1)

            def statistics(tiles, srcs, signal):
                for t, src in zip(tiles, srcs):
                    v.bn_stats(STAT[:, t], src).then_inc(S["dve_own"], 1)
                    own.n += 1
                wait_apart(dve, (S["dve_own"], own.base + own.n))
                for t in tiles:
                    v.bn_aggr(MV[:, t], STAT[:, t]).then_inc(S["dve_own"], 1)
                    own.n += 1
                dve.wait_ge(S["dve_own"], own.base + own.n)
                sl = slice(tiles[0], tiles[-1] + 1)
                v.tensor_scalar(VE[:, sl], MV[:, sl, 1], NORM_EPS, None, ALU.add).then_inc(S[signal], 1)

            def centred(dst, src, t):
                return v.tensor_scalar(dst, src, MV[:, t, 0:1], RSTD[:, t:t + 1], ALU.subtract, ALU.mult)

            own(v.memset(NW[:], 0.0))
            own(v.memset(DW[:], 0.0))
            with dve.Fori(0, B) as b:
                own.enter(b, PER_B)

                def first_statistics(t, par):
                    v.bn_stats(STAT1[:, par], X[:, bass.ds(t, 1)].rearrange("p t d -> p (t d)")
                               ).then_inc(S["dve_own"], 1)
                    own.n += 1
                    wait_apart(dve, (S["dve_own"], own.base + own.n))
                    own(v.bn_aggr(MV1[:, par], STAT1[:, par]))
                    v.tensor_scalar(VE1[:, par:par + 1], MV1[:, par, 1:2], NORM_EPS, None, ALU.add
                                    ).then_inc(S["ve1"], 1)

                def first_norm(t, par, at):
                    n = b * NT + t
                    wait_apart(dve, (S["rstd1"], n + 1))
                    if at >= 2:
                        dve.wait_ge(S["xT"], n - 1)
                    v.tensor_scalar(XH[:, par], X[:, bass.ds(t, 1)].rearrange("p t d -> p (t d)"), MV1[:, par, 0:1],
                                    RSTD1[:, par:par + 1], ALU.subtract, ALU.mult).then_inc(S["xh"], 1)

                def low_qk(t):
                    n = b * NT + t
                    dve.wait_ge(S["qkT_sb"], n + 1)
                    v.tensor_tensor(QKT[:, 1].rearrange("p a n -> p (a n)"), bank(4),
                                    QKT[:, 0].bitcast(F32).rearrange("p a n -> p (a n)"), ALU.subtract
                                    ).then_inc(S["qkT_lo"], 1)

                def norms(t, par):
                    dve.wait_ge(S["sq"], b * NT + t + 1)
                    v.tensor_reduce(N2[:, par], SQ[:].rearrange("p (h d) -> p h d", d=DK), AX.X, ALU.add
                                    ).then_inc(S["n2"], 1)

                def shifted(n, at, src, mx, dst, n2, ready, read_by, read_count, signal, between=None):
                    dve.wait_ge(ready, n + 1)
                    sc = src.rearrange("p (h m) -> p h m", m=NM)
                    own(v.tensor_reduce(mx[:], sc, AX.X, ALU.max))
                    dve.wait_ge(S["n2"], n + 1)
                    own(v.scalar_tensor_tensor(mx[:], n2, 0.5, mx[:], ALU.mult, ALU.add))
                    if between is not None:
                        between()
                    if at >= 1:
                        dve.wait_ge(read_by, read_count)
                    v.tensor_tensor(dst[:].rearrange("p (h m) -> p h m", m=NM), sc,
                                    mx[:].rearrange("p (h o) -> p h o", o=1).broadcast_to([P, NH, NM]),
                                    ALU.subtract).then_inc(signal, 1)

                dve.wait_ge(S["x_first"], 16 * (b + 1))
                first_statistics(0, 0)
                first_statistics(1, 1)
                first_norm(0, 0, 0)
                first_statistics(2, 0)
                norms(0, 0)
                first_norm(1, 1, 1)
                low_qk(0)

                def tile(t, par, at):
                    n = b * NT + t
                    shifted(n, at, bank(0, 2), MXK, XSK, N2[:, par, NH:], S["xwk"], S["phik"], n, S["xk_sb"])
                    if at < NT - 2:
                        first_norm(t + 2, par, at + 2)
                    if at == 1:
                        dve.wait_ge(S["x_rest"], 16 * (NC - 1) * (b + 1))
                    if at < NT - 3:
                        first_statistics(t + 3, 1 - par)
                    shifted(n, at, bank(2, 2), MXQ, XSQ, N2[:, par, :NH], S["xwq"], S["eqt"], 2 * n, S["xq_sb"],
                            (lambda: low_qk(t + 1)) if at < NT - 1 else None)
                    if at < NT - 1:
                        norms(t + 1, 1 - par)

                over_tiles(dve, tile, own)
                dve.wait_ge(S["kv"], NT * (b + 1))
                v.tensor_copy(DENS[:], bank(7)).then_inc(S["kv_sb"], 1)
                dve.wait_ge(S["kvT"], b + 1)
                kvt = bank(6).rearrange("p (a g n) -> p a g n", a=2, g=GR)
                for half, r in ((0, slice(0, NM)), (1, slice(NM, P))):
                    cols = slice(half * DK, (half + 1) * DK)
                    v.tensor_copy(NW[r, :, cols], kvt[r, 0, :, cols]).then_inc(S["kw_ok"], 1)
                    for j in range(2):
                        c = 2 * j + half
                        v.tensor_copy(DW[r, 4 * j:4 * j + 4, c:c + 1], kvt[r, 1, 4 * j:4 * j + 4, 0:1]
                                      ).then_inc(S["kw_ok"], 1)
                own(v.memset(MXN[:], 0.0))

                def maxima(p0, p1):
                    for p in range(p0, min(p1, NU * MAXU)):
                        u, i, kc = stream[p]
                        dve.wait_ge(S["am"], NU * MAXU * b + p + 1)
                        v.tensor_reduce(MXP[:, u % 2, i, kc:kc + 1], bank(max_bank(p)), AX.X, ALU.max
                                        ).then_inc(S["am_rd"], 1)
                        if p == last_of[u]:
                            dve.wait_ge(S["am_rd"], NU * MAXU * b + p + 1)
                            own(v.tensor_reduce(MXN[:, u % 2, 0:TPC], MXP[:, u % 2], AX.X, ALU.max, negate=True))
                            if u >= 2:
                                dve.wait_ge(shift[(u - 2) % 4], 64 * (SHN[(u - 2) % 4] * b + (u - 2) // 4 + 1))
                            v.transpose(MXT[:, u % 2], MXN[:, u % 2]).then_inc(S["mxt"], 1)

                for it in range(NC + 3):
                    g = b * NC + it
                    if it < NC:
                        dve.wait_ge(S["denT"], g + 1)
                        if it > 0:
                            dve.wait_ge(S["rb"], 2 * g)
                        for j in range(2):
                            v_ins = v.tensor_scalar(R[:, :, j], bank(7).rearrange("p (i q n) -> p i q n", i=TPC, q=4)
                                                    [:, :, :, 2 * j:2 * j + 2], FAVOR_EPS, None, ALU.add)
                            own(v_ins)
                        v.reciprocal(R[:], R[:]).then_inc(S["rec"], 1)
                    if 1 <= it <= NC:
                        dve.wait_ge(S["rstd2"], g)
                        for i in range(TPC):
                            t = (it - 1) * TPC + i
                            v_ins = centred(Hh[:, t], X[:, t], t)
                            if i < TPC - 1:
                                own(v_ins)
                        v_ins.then_inc(S["h2a"], 1)
                    if it < NC:
                        if it > 0:
                            dve.wait_ge(S["yps"], 2 * g)
                        for i2 in range(2):
                            half = slice(i2 * 2 * P, (i2 + 1) * 2 * P)
                            dve.wait_ge(S["rT"], 2 * g + i2 + 1)
                            dve.wait_ge(S["num_sb"], 2 * g + 2)
                            v.tensor_tensor(MT[:, :, half], bank(4 + i2).rearrange("p (j n) -> p j n", j=2), NUMS[:, :, half], ALU.mult
                                            ).then_inc(S["mt"], 1)
                    if 2 <= it < NC + 2:
                        dve.wait_ge(S["rstd3"], g - 1)
                        if it > 2:
                            dve.wait_ge(S["x2T"], g - 2)
                        for i in range(TPC):
                            t = (it - 2) * TPC + i
                            m = D if expert[it - 2] == 0 else P
                            centred(X2[:, i, 0:m], Hh[:, t, 0:m], t).then_inc(S["x2"], 1)
                    if it >= 3:
                        for n, t in blocks(it - 3):
                            dve.wait_ge(S["q_hi"], NQ * b + n + 1)
                            v.tensor_tensor(QKS[:, n % 3, 1], TMP[:, n % 2], QKS[:, n % 3, 0].bitcast(F32),
                                            ALU.subtract).then_inc(S["q_lo"], 1)
                    if it >= 3:
                        for i2 in range(2):
                            dve.wait_ge(S["vp"], 2 * (NC * b + it - 3) + i2 + 1)
                            t = expert[it - 3] * TPC + 2 * i2
                            v.tensor_tensor(V2[:, t:t + 2], bank(i2).rearrange("p (t d) -> p t d", t=2),
                                            VB[:].rearrange("p (o d) -> p o d", o=1).broadcast_to([P, 2, D]), ALU.add
                                            ).then_inc(S["v2_sb"], 1)
                    if it == NC:
                        dve.wait_ge(S["h2a"], g)
                        for op, m in ((ALU.mult, 2), (ALU.add, 1)):
                            own(v.tensor_tensor(Hh[:, slot(NC - 1)], Hh[:, slot(NC - 1)],
                                                MODB[:, bass.ds(b, 1), m, :].broadcast_to([P, TPC, D]), op))
                    if it in (4, 5):
                        maxima((it - 4) * EARLY, (it - 3) * EARLY)
                    if it < NC:
                        if it == 0:
                            dve.wait_ge(S["xb"], NT * (b + 1))
                        for i2 in range(2):
                            dve.wait_ge(S["yps"], 2 * g + i2 + 1)
                            half = slice(it * TPC + 2 * i2, it * TPC + 2 * i2 + 2)
                            v.tensor_tensor(X[:, half], bank(6 + i2).rearrange("p (t d) -> p t d", t=2), X[:, half],
                                            ALU.add).then_inc(S["x1"], 1)
                        dve.wait_ge(S["x1"], 2 * (g + 1))
                        statistics(range(it * TPC, (it + 1) * TPC), [X[:, it * TPC + i] for i in range(TPC)], "ve2")
                    if 1 <= it <= NC:
                        if it < NC:
                            dve.wait_ge(S["h2"], (NC - 1) * b + it)
                        statistics(range((it - 1) * TPC, it * TPC), [Hh[:, (it - 1) * TPC + i] for i in range(TPC)], "ve3")

                def divide_part(z, q):
                    part = SUM[:, z, q * P:(q + 1) * P]
                    return v.reciprocal(part, part)

                def result(k):
                    e = results[k]
                    s, m = slot_of[e], width[e]
                    src = out_ps(e).rearrange("p (t d) -> p t d", t=TPC)
                    dve.wait_ge(S["ops"], b * NC + k + 1)
                    dve.wait_ge(S["base"], b * NC + k + 1)
                    v.tensor_tensor(X[:, slot(s), 0:m], src, X[:, slot(s), 0:m], ALU.add).then_inc(S["fin"], 1)

                maxima(2 * EARLY, LOOK)
                own(v.memset(NUM[2 * DH:, 2:4], 0.0))
                own(v.memset(NUM[DH:2 * DH, 3], 0.0))
                own(v.memset(SUM[2 * DH:, 2:4], 1.0))
                own(v.memset(SUM[DH:2 * DH, 3], 1.0))
                for u, (h, c) in enumerate(units):
                    for s in range(STEPS):
                        p = u * MAXU + s * 2 + LOOK
                        maxima(p, p + 2)
                        if s == 2 and u > 0:
                            finish(dve, v, b, u - 1)
                        for z, at in RECIPROCALS:
                            if u == at and s >= 4:
                                if s == 4:
                                    dve.wait_ge(S["c_out"], NU * b + u)
                                divide_part(z, s - 4).then_inc(S["rcp"], 1)
                        if u == NU - 1 and s in OUT_STEPS:
                            result(OUT_STEPS.index(s))
                finish(dve, v, b, NU - 1)
                dve.wait_ge(S["c_out"], NU * (b + 1))
                dve.wait_ge(S["fin_n"], NU * (b + 1))
                for q in range(TPC):
                    own(divide_part(NC, q))
                    part = slice(q * P, (q + 1) * P)
                    v.tensor_tensor(NUM[:, NC, part], NUM[:, NC, part], SUM[:, NC, part], ALU.mult
                                    ).then_inc(S["at_last"], 1)
                result(NC - 1)
                wait_apart(dve, (S["fin"], NC * (b + 1)))
                own.leave(B)

        @block.tensor
        def _(pe):
            mm, tr = nc.tensor.matmul, nc.tensor.transpose
            pe.wait_ge(S["id_ok"], 1)
            pe.wait_ge(S["w_in"], 16 * 8)
            for w in range(8):
                for k in range(KD):
                    for e in range(KD):
                        last = tr(bank(w)[:, k * D + e * P:k * D + (e + 1) * P], WN[:, w, e, k * P:(k + 1) * P], ident[:])
                last.then_inc(S["wT"], 1)
            pe.wait_ge(S["pj_in"], 16 * NH)
            for j in range(2):
                pe.wait_ge(S["wT_sb"], j + 1)
                for q in range(4):
                    last = tr(bank(j)[:, q * P:(q + 1) * P], PN[:, 4 * j + q], ident[:])
                last.then_inc(S["pT"], 1)
            pe.wait_ge(S["c_in"], 16 * (1 + KD))
            pe.wait_ge(S["sc_ok"], KD * B)
            pe.wait_ge(S["wT_sb"], 3)
            for m in range(2):
                for e in range(KD):
                    o = (m * KD + e) * B
                    for k in range(KD):
                        last = mm(bank(2)[:, o:o + B], WM[:, k, m * D + e * P:m * D + (e + 1) * P], SC[:, k],
                                  start=k == 0, stop=k == KD - 1)
            last.then_inc(S["mod"], 1)
            for b in range(B):
                pe.wait_ge(S["wT_sb"], 8)
                if b >= 2:
                    pe.wait_ge(S["mod_sb"], b - 1)
                for q in range(2):
                    for k in range(KD):
                        last = mm(bank(4 + b % 2 * 2 + q), SCB[:, k, b], WM[:, k, (q + 1) * CH:(q + 2) * CH],
                                  start=k == 0, stop=k == KD - 1)
                last.then_inc(S["mod"], 1)
            pe.wait_ge(S["setup_ok"], 1)

            with pe.Fori(0, B) as b:
                def x_transposes(t, par, at):
                    n = b * NT + t
                    pe.wait_ge(S["xh"], n + 1)
                    if at >= 1:
                        pe.wait_ge(S["v_sb"], n)
                    for k in range(KD):
                        last = tr(bank(6)[:, D + k * P:D + (k + 1) * P], XH[:, par, k * P:(k + 1) * P], ident[:])
                    last.then_inc(S["xT"], 1)

                def project(t, at):
                    n = b * NT + t
                    pe.wait_ge(S["hT_lo"], n + 1)
                    if at >= 1:
                        pe.wait_ge(S["qkT_lo"], n)
                    for m, (x_, w_) in enumerate(PARTS):
                        for k in range(KD):
                            mm(bank(4), HTR[:, x_, k], W1T[:, w_, k], start=m == 0 and k == 0,
                               stop=m == len(PARTS) - 1 and k == KD - 1)
                    pe.wait_ge(S["hT"], KD * (n + 1))
                    for k in range(KD):
                        last = mm(bank(6)[:, 0:D], HT[:, k], WvT[:, k], start=k == 0, stop=k == KD - 1)
                    last.then_inc(S["qkv"], 1)

                def qk_transposes(t, at):
                    n = b * NT + t
                    pe.wait_ge(S["qk_sb"], n + 1)
                    pe.wait_ge(S["sq"], n + 1)
                    for q in range(4):
                        last = tr(bank(4)[:, q * P:(q + 1) * P], QK[:, q * P:(q + 1) * P], ident[:])
                    last.then_inc(S["qkT"], 1)

                def query_features(t, half, at):
                    n = b * NT + t
                    if half == 0:
                        pe.wait_ge(S["expq"], n + 1)
                        if at >= 1:
                            pe.wait_ge(S["phiq"], 2 * n)
                    else:
                        pe.wait_ge(S["phiq"], 2 * n + 1)
                    for q in range(4):
                        last = tr(bank(5)[:, q * P:(q + 1) * P], XSQ[:, (half * 4 + q) * P:(half * 4 + q + 1) * P], ident[:])
                    last.then_inc(S["eqt"], 1)

                def scores(n, at, base, o, ready, free):
                    if at >= 1:
                        pe.wait_ge(S[free], n)
                    for j in range(2):
                        for m, (x_, w_) in enumerate(PARTS):
                            last = mm(bank(base + j), QKT[:, x_, o + j], PB[:, w_, j], start=m == 0,
                                      stop=m == len(PARTS) - 1)
                    last.then_inc(S[ready], 1)

                def key_values(n, par, at):
                    pe.wait_ge(S["phik"], n + 1)
                    for a_ in range(2):
                        for j in range(2):
                            for q in range(4):
                                gr = 4 * j + q
                                W = V1[:, par, gr * 2 * DK:(gr + 1) * 2 * DK] if a_ == 0 else ones[:]
                                last = mm(bank(7)[32 * q:32 * q + 32, (2 * a_ + j) * P:(2 * a_ + j + 1) * P], W,
                                          PK[:, par, gr * P:(gr + 1) * P], start=at == 0 and a_ == 0 and j == 0,
                                          stop=at == NT - 1, skip_group_check=True, tile_position=(0, 32 * q))
                    last.then_inc(S["kv"], 1)

                x_transposes(0, 0, 0)
                project(0, 0)
                qk_transposes(0, 0)
                x_transposes(1, 1, 1)

                def tile(t, par, at):
                    n = b * NT + t
                    pe.wait_ge(S["qkT_lo"], n + 1)
                    scores(n, at, 0, 2, "xwk", "xk_sb")
                    if at >= 1:
                        query_features(t - 1, 0, at - 1)
                    if at < NT - 1:
                        project(t + 1, at + 1)
                    scores(n, at, 2, 0, "xwq", "xq_sb")
                    if at >= 1:
                        query_features(t - 1, 1, at - 1)
                    if at < NT - 1:
                        qk_transposes(t + 1, at + 1)
                    if at < NT - 2:
                        x_transposes(t + 2, par, at + 2)
                    key_values(n, par, at)

                over_tiles(pe, tile)
                query_features(NT - 1, 0, NT - 1)
                query_features(NT - 1, 1, NT - 1)
                pe.wait_ge(S["kv_sb"], b + 1)
                pe.wait_ge(S["v_sb"], NT * (b + 1))
                for a_ in range(2):
                    for j in range(2):
                        last = tr(bank(6)[:, (2 * a_ + j) * P:(2 * a_ + j + 1) * P], KVS[:, a_, j], ident[:])
                last.then_inc(S["kvT"], 1)
                pe.wait_ge(S["kw_ok"], 6 * (b + 1))
                pe.wait_ge(S["phiq"], 2 * NT * (b + 1))
                pe.wait_ge(S["xq_sb"], NT * (b + 1))

                def maxima(p0, p1):
                    for p in range(p0, min(p1, NU * MAXU)):
                        u, i, kc = stream[p]
                        h, c = units[u]
                        if p == stream.index((u, 0, expert[0] if u < 2 else 0)):
                            pe.wait_ge(q_in[u % 4], 48 * (SHN[u % 4] * b + u // 4 + 1))
                            if h > 0:
                                pe.wait_ge(*keys_there(b, h))
                        if u == 0 and i == 0:
                            pe.wait_ge(S[f"kf{kc}"], 48 * (b + 1))
                        if p == 0:
                            pe.wait_ge(S["x1"], 2 * NC * (b + 1))
                        back = 2 if p >= LOOK else 4
                        if p >= back:
                            pe.wait_ge(S["am_rd"], NU * MAXU * b + p - back + 1)
                        mm(bank(max_bank(p)), QOP[0:96, u % 4, i * P:(i + 1) * P],
                           KOP[0:96, heads.index(h) % 4, kc * CH:(kc + 1) * CH], start=True, stop=True
                           ).then_inc(S["am"], 1)

                for it in range(NC + 3):
                    g = b * NC + it
                    if it < NC:
                        cols = slice(it * CH, (it + 1) * CH)
                        if it > 0:
                            pe.wait_ge(S["x1"], 2 * g - 1)
                        for j in range(2):
                            for q in range(4):
                                last = mm(bank(6)[32 * q:32 * q + 32, :], DW[:, 4 * j + q], PHIQ[:, 4 * j + q, cols],
                                          start=j == 0, stop=j == 1, tile_position=(0, 32 * q))
                        last.then_inc(S["den"], 1)
                        for j in range(2):
                            if it > 0 and j == 0:
                                pe.wait_ge(S["mt"], 2 * g)
                            for q in range(4):
                                last = mm(bank(4 + j)[32 * q:32 * q + 32, :], NW[:, 4 * j + q],
                                          PHIQ[:, 4 * j + q, cols], start=True, stop=True,
                                          tile_position=(0, 32 * q))
                            last.then_inc(S["num"], 1)
                            if j == 0:
                                pe.wait_ge(S["den_sb"], g + 1)
                                if it > 0:
                                    pe.wait_ge(S["x1"], 2 * g)
                                for i in range(TPC):
                                    last = tr(bank(7)[:, i * P:(i + 1) * P], DENS[:, i * P:(i + 1) * P], ident[:])
                                last.then_inc(S["denT"], 1)
                    if it >= 3:
                        s = it - 3
                        e = expert[s]
                        ks = range(KD if e == 0 else 1)
                        pe.wait_ge(S["xn_sb"], (NC + 1) * b + s + (2 if s >= slot_of[0] else 1))
                        for n, t in blocks(s):
                            j, w = t % 2, (1 if t < 2 else 0)
                            if n >= 2:
                                pe.wait_ge(S["q_hi"], NQ * b + n - 1)
                            for k in ks:
                                last = mm(bank(2 + n % 2), W2T[:, k, w * D + j * P:w * D + (j + 1) * P], XNT[:, k],
                                          start=k == 0, stop=k == len(ks) - 1)
                            last.then_inc(S["qp"], 1)
                    if it < NC:
                        for i in range(TPC):
                            for j in range(2):
                                if i % 2 == 0 and j == 0:
                                    pe.wait_ge(S["num_sb"], 2 * g + i // 2 + 1)
                                    pe.wait_ge(S["rb"], 2 * g + i // 2 + 1)
                                last = tr(bank(4 + i // 2)[:, (2 * j + i % 2) * P:][:, 0:P], RB[:, i, j], ident[:])
                            if i % 2 == 1:
                                last.then_inc(S["rT"], 1)
                    if it >= 3:
                        for i in range(TPC):
                            for k in ks:
                                last = mm(bank(i // 2)[:, i % 2 * D:(i % 2 + 1) * D], XNT[:, k, i * P:(i + 1) * P], W2T[:, k, 2 * D:],
                                          start=k == 0, stop=k == len(ks) - 1)
                            if i % 2 == 1:
                                last.then_inc(S["vp"], 1)
                    if it < NC:
                        pe.wait_ge(S["gated"], 2 * (b + 1))
                        for i in range(TPC):
                            if i % 2 == 0:
                                pe.wait_ge(S["mt"], 2 * g + i // 2 + 1)
                            for j in range(2):
                                last = mm(bank(6, 2)[:, i * D:(i + 1) * D], MT[:, j, i * P:(i + 1) * P], WoG[:, j],
                                          start=j == 0, stop=j == 1)
                            if i % 2 == 1:
                                last.then_inc(S["yps"], 1)
                    if 2 <= it < NC + 2:
                        pe.wait_ge(S["x2"], (g - 1) * TPC)
                        if it >= 3:
                            pe.wait_ge(S["v2_sb"], (g - 2) * 2)
                        for i in range(TPC):
                            for k in range(KD if expert[it - 2] == 0 else 1):
                                last = tr(bank(k)[:, i * P:(i + 1) * P], X2[:, i, k * P:(k + 1) * P], ident[:])
                        last.then_inc(S["x2T"], 1)
                    if it in (4, 5):
                        maxima((it - 4) * EARLY, (it - 3) * EARLY)

                pe.wait_ge(S["q_hi"], NQ * (b + 1))
                pe.wait_ge(S["v2_sb"], 2 * NC * (b + 1))

                def output(k):
                    e = results[k]
                    m = width[e]
                    pe.wait_ge(S["at"], len(RECIPROCALS) * b + [z for z, _ in RECIPROCALS].index(e) + 1)
                    if e == 1:
                        pe.wait_ge(S["am_rd"], NU * MAXU * (b + 1))
                        pe.wait_ge(S["base"], NC * b + 1)
                    if e == 3:
                        pe.wait_ge(S["fin"], NC * b + 2)
                    for i in range(TPC):
                        o = out_ps(e)[:, i * m:(i + 1) * m]
                        last = mm(o, NUM[:, e, i * P:(i + 1) * P],
                                  OWG[:, 0, 0:m], start=True, stop=True)
                    last.then_inc(S["ops"], 1)

                def values(u, s):
                    h, c = units[u]
                    pe.wait_ge(S["ex"], (NU * b + u) * STEPS + s + 1)
                    if s == 0 and u >= 2:
                        pe.wait_ge(S["c_out"], NU * b + u - 1)
                    for q in range(2):
                        kt = 2 * s + q
                        for z, W in ((0, V2[:, kt, h * DH:(h + 1) * DH]), (1, ones[:])):
                            r = 64 * q + 32 * z
                            last = mm(PS[r:r + DH, 6 + u % 2, :], W, PR[:, s % 2, q], start=s == 0,
                                      stop=s == STEPS - 1, tile_position=(0, r))
                    if s == STEPS - 1:
                        last.then_inc(S["cps"], 1)

                maxima(2 * EARLY, LOOK)
                for u, (h, c) in enumerate(units):
                    ks = heads.index(h) % 4
                    pe.wait_ge(shift[u % 4], 64 * (SHN[u % 4] * b + u // 4 + 1))
                    for s in range(STEPS):
                        for q in range(2):
                            kt = 2 * s + q
                            last = mm(bank(2 + s % 2 * 2 + q), KOP[:, ks, kt * P:(kt + 1) * P], QOP[:, u % 4],
                                      start=True, stop=True)
                        last.then_inc(S["sc_b"], 1)
                        p = u * MAXU + s * 2 + LOOK
                        maxima(p, p + 2)
                        if s > 0:
                            values(u, s - 1)
                        elif u > 0:
                            values(u - 1, STEPS - 1)
                        if u == NU - 1 and s in OUT_STEPS:
                            output(OUT_STEPS.index(s))
                values(NU - 1, STEPS - 1)
                pe.wait_ge(S["ex"], NU * STEPS * (b + 1))
                pe.wait_ge(S["at"], len(RECIPROCALS) * (b + 1))
                for i in range(TPC):
                    tok = slice(i * P, (i + 1) * P)
                    o = out_ps(0)[:, i * D:(i + 1) * D]
                    mm(o, NUM[:, 0, tok], OWG[:, 0], start=True, stop=False)
                    pe.wait_ge(S["at_last"], TPC * b + i + 1)
                    last = mm(o, NUM[:, NC, tok], OWG[:, 1], start=False, stop=True)
                last.then_inc(S["ops"], 1)


_INS = ['L0_attn_x', 'L0_attn_Wq', 'L0_attn_Wk', 'L0_attn_Wv', 'L0_attn_Wo', 'L0_attn_bo', 'L0_attn_proj',
        'L0_ffn_norm_w', 'L0_ffn_norm_b', 'L0_ffn_q_w', 'L0_ffn_q_b', 'L0_ffn_k_w', 'L0_ffn_k_b',
        'L0_ffn_v_w', 'L0_ffn_v_b', 'L0_ffn_o_w', 'L0_ffn_o_b', 'L0_c', 'L0_wmod']


def kernel(**inputs):
    import numpy as _np
    import concourse.bacc as _bacc
    from concourse import mybir as _mybir
    from concourse.bass_utils import run_bass_kernel_spmd as _run

    nc = _bacc.Bacc("TRN2", target_bir_lowering=False, num_devices=1)
    arrays, args = {}, []
    for name in _INS:
        a = _np.ascontiguousarray(inputs[name])
        arrays[f"in_{name}_dram"] = a
        args.append(nc.dram_tensor(f"in_{name}_dram", a.shape, _mybir.dt.from_np(a.dtype), kind="ExternalInput").ap())
    out = nc.dram_tensor("out_0_dram", inputs['L0_attn_x'].shape, F32, kind="ExternalOutput").ap()
    adaln_block(nc, *args, out)
    r = _run(nc, [arrays], core_ids=[0])
    return r.results[0]["out_0_dram"]
```
